# Optimizing a Trainium2 kernel written in Bass

```python
import numpy as np
import jax
import jax.numpy as jnp

def _softmax(x, axis=-1):
    return jax.nn.softmax(x, axis=axis)

def _gelu(x):
    return jax.nn.gelu(x, approximate=True)

def _silu(x):
    return jax.nn.silu(x)

def _sigmoid(x):
    return jax.nn.sigmoid(x)

def _layernorm(x, axis=-1, eps=1e-05):
    m = jnp.mean(x, axis=axis, keepdims=True)
    v = jnp.var(x, axis=axis, keepdims=True)
    return (x - m) / jnp.sqrt(v + eps)

def _scatter_add(tgt, idx, src, axis=0):
    return tgt.at[idx].add(src)

def _segment_sum(src, seg, n):
    return jax.ops.segment_sum(src, seg, n)
kernel_name = 'mk_gnn_resnorm_d4_gnn_r64_b25edf'

def setup_inputs(seed: int=0):
    np.random.seed(seed)
    _w = jnp.asarray

    def _rec_inputs():
        import jax
        import jax.numpy as jnp
        _gk = jax.random.key(seed)
        x = -0.0002117 + 1 * jax.random.normal(jax.random.fold_in(_gk, 1), (100000, 256), jnp.float32)
        src = jax.random.randint(jax.random.fold_in(_gk, 2), (25000,), 0, 100000, jnp.int32)
        dst = jax.random.randint(jax.random.fold_in(_gk, 3), (25000,), 0, 100000, jnp.int32)
        _o = jnp.argsort(dst, stable=True)
        src = src[_o]
        dst = dst[_o]
        edge_weight = jax.random.uniform(jax.random.fold_in(_gk, 13), (25000,), jnp.float32, 0.0, 1)
        return (x, src, dst, edge_weight)
    x, src, dst, edge_weight = _rec_inputs()

    def _L0_gnn_setup():
        import jax, jax.numpy as jnp
        import numpy as np
        N = 100000
        E = 12500
        IN = 256
        H = 8
        D = 32
        HD = H * D
        HID = 128
        NEG_SLOPE = 0.2

        def _gat(h, W_fc, attn_l, attn_r, bias, src, dst):
            feat = (h @ W_fc).reshape(N, H, D)
            el = jnp.sum(feat * attn_l, axis=-1)
            er = jnp.sum(feat * attn_r, axis=-1)
            e = jax.nn.leaky_relu(el[src] + er[dst], NEG_SLOPE)
            mx = jax.ops.segment_max(e, dst, num_segments=N)
            mx = jnp.where(jnp.isfinite(mx), mx, 0.0)
            ee = jnp.exp(e - mx[dst])
            denom = jax.ops.segment_sum(ee, dst, num_segments=N)
            alpha = ee / denom[dst]
            msg = feat[src] * alpha[:, :, None]
            rst = jax.ops.segment_sum(msg, dst, num_segments=N)
            rst = rst + bias.reshape(H, D)
            return jax.nn.elu(rst).reshape(N, HD)
        key = jax.random.key(seed)
        ks = jax.random.split(key, 10)
        h = jax.random.normal(ks[0], (N, IN), dtype=jnp.float32)
        src = jax.random.randint(ks[1], (E,), 0, N)
        dst = jax.random.randint(ks[2], (E,), 0, N)
        s = 0.05
        W_fc = jax.random.normal(ks[3], (IN, HD), dtype=jnp.float32) * s
        attn_l = jax.random.normal(ks[4], (H, D), dtype=jnp.float32) * s
        attn_r = jax.random.normal(ks[5], (H, D), dtype=jnp.float32) * s
        bias = jnp.zeros((HD,), dtype=jnp.float32)
        sem_W1 = jax.random.normal(ks[6], (HD, HID), dtype=jnp.float32) * s
        sem_b1 = jnp.zeros((HID,), dtype=jnp.float32)
        sem_W2 = jax.random.normal(ks[7], (HID, 1), dtype=jnp.float32) * s
        return {'h': h, 'W_fc': W_fc, 'attn_l': attn_l, 'attn_r': attn_r, 'bias': bias, 'sem_W1': sem_W1, 'sem_b1': sem_b1, 'sem_W2': sem_W2, 'src': src, 'dst': dst}
    _L0_gnn_all = _L0_gnn_setup()
    _L0_gnn_in = {k: v for k, v in _L0_gnn_all.items() if k in ('W_fc', 'attn_l', 'attn_r', 'bias', 'sem_W1', 'sem_b1', 'sem_W2')}
    del _L0_gnn_all

    def _L1_gnn_setup():
        import jax, jax.numpy as jnp
        import numpy as np
        N = 100000
        E = 50000
        D_IN = 256
        D_OUT = 256
        key = jax.random.key(seed)
        k_x, k_w, k_r, k_c, k_v = jax.random.split(key, 5)
        x = jax.random.normal(k_x, (N, D_IN), dtype=jnp.float32)
        W = jax.random.normal(k_w, (D_OUT, D_IN), dtype=jnp.float32) / np.sqrt(D_IN)
        edge_row = jax.random.randint(k_r, (E,), 0, N, dtype=jnp.int32)
        edge_col = jax.random.randint(k_c, (E,), 0, N, dtype=jnp.int32)
        edge_val = jax.random.uniform(k_v, (E,), dtype=jnp.float32)
        return {'x': x, 'W': W, 'edge_row': edge_row, 'edge_col': edge_col, 'edge_val': edge_val}
    _L1_gnn_all = _L1_gnn_setup()
    _L1_gnn_in = {k: v for k, v in _L1_gnn_all.items() if k in ('W',)}
    del _L1_gnn_all

    def _L2_gnn_setup():
        import jax, jax.numpy as jnp
        import numpy as np
        N_NODES = 50000
        N_EDGES = 12500
        IN_CH = 256
        HEADS = 8
        HEAD_DIM = 32
        NEG_SLOPE = 0.2
        LN_EPS = 1e-05
        SOFTMAX_EPS = 1e-16
        key = jax.random.key(seed)
        k1, k2, k3, k4 = jax.random.split(key, 4)
        x = jax.random.normal(k1, (N_NODES, IN_CH), dtype=jnp.float32)
        edge_index = jax.random.randint(k2, (2, N_EDGES), 0, N_NODES, dtype=jnp.int64)
        lin_w = jax.random.normal(k3, (IN_CH, HEADS * HEAD_DIM), dtype=jnp.float32) * (1.0 / np.sqrt(IN_CH))
        att = jax.random.normal(k4, (HEADS, 2 * HEAD_DIM), dtype=jnp.float32) * 0.1
        ln_w = jnp.ones((HEADS * HEAD_DIM,), dtype=jnp.float32)
        ln_b = jnp.zeros((HEADS * HEAD_DIM,), dtype=jnp.float32)
        return {'x': x, 'edge_index': edge_index, 'lin_w': lin_w, 'att': att, 'ln_w': ln_w, 'ln_b': ln_b}
    _L2_gnn_all = _L2_gnn_setup()
    _L2_gnn_in = {k: v for k, v in _L2_gnn_all.items() if k in ('lin_w', 'att', 'ln_w', 'ln_b')}
    del _L2_gnn_all

    def _L3_gnn_setup():
        import jax, jax.numpy as jnp
        import numpy as np
        N_NODES = 100000
        N_EDGES = 50000
        IN_FEATS = 256
        OUT_FEATS = 256
        key = jax.random.key(seed)
        k1, k2, k3, k4, k5, k6 = jax.random.split(key, 6)
        features = jax.random.normal(k1, (N_NODES, IN_FEATS), dtype=jnp.float32)
        edge_src = jax.random.randint(k2, (N_EDGES,), 0, N_NODES, dtype=jnp.int64)
        edge_dst = jnp.sort(jax.random.randint(k3, (N_EDGES,), 0, N_NODES, dtype=jnp.int64))
        edge_weight = jax.random.uniform(k4, (N_EDGES,), dtype=jnp.float32)
        bound = 1.0 / np.sqrt(IN_FEATS)
        W = jax.random.uniform(k5, (OUT_FEATS, IN_FEATS), dtype=jnp.float32, minval=-bound, maxval=bound)
        b = jax.random.uniform(k6, (OUT_FEATS,), dtype=jnp.float32, minval=-bound, maxval=bound)
        return {'features': features, 'edge_src': edge_src, 'edge_dst': edge_dst, 'edge_weight': edge_weight, 'W': W, 'b': b}
    _L3_gnn_all = _L3_gnn_setup()
    _L3_gnn_in = {k: v for k, v in _L3_gnn_all.items() if k in ('W', 'b')}
    del _L3_gnn_all
    return {'x': x, 'src': src, 'dst': dst, 'edge_weight': edge_weight, 'L0_gnn_W_fc': _L0_gnn_in['W_fc'], 'L0_gnn_attn_l': _L0_gnn_in['attn_l'], 'L0_gnn_attn_r': _L0_gnn_in['attn_r'], 'L0_gnn_bias': _L0_gnn_in['bias'], 'L0_gnn_sem_W1': _L0_gnn_in['sem_W1'], 'L0_gnn_sem_b1': _L0_gnn_in['sem_b1'], 'L0_gnn_sem_W2': _L0_gnn_in['sem_W2'], 'L1_gnn_W': _L1_gnn_in['W'], 'L2_gnn_lin_w': _L2_gnn_in['lin_w'], 'L2_gnn_att': _L2_gnn_in['att'], 'L2_gnn_ln_w': _L2_gnn_in['ln_w'], 'L2_gnn_ln_b': _L2_gnn_in['ln_b'], 'L3_gnn_W': _L3_gnn_in['W'], 'L3_gnn_b': _L3_gnn_in['b']}

def reference(x, src, dst, edge_weight, L0_gnn_W_fc, L0_gnn_attn_l, L0_gnn_attn_r, L0_gnn_bias, L0_gnn_sem_W1, L0_gnn_sem_b1, L0_gnn_sem_W2, L1_gnn_W, L2_gnn_lin_w, L2_gnn_att, L2_gnn_ln_w, L2_gnn_ln_b, L3_gnn_W, L3_gnn_b):
    import jax
    import jax.numpy as jnp

    def _L0_gnn_ref(h, W_fc, attn_l, attn_r, bias, sem_W1, sem_b1, sem_W2, src, dst):
        import jax, jax.numpy as jnp
        import numpy as np
        N = 100000
        E = 12500
        IN = 256
        H = 8
        D = 32
        HD = H * D
        HID = 128
        NEG_SLOPE = 0.2

        def _gat(h, W_fc, attn_l, attn_r, bias, src, dst):
            feat = (h @ W_fc).reshape(N, H, D)
            el = jnp.sum(feat * attn_l, axis=-1)
            er = jnp.sum(feat * attn_r, axis=-1)
            e = jax.nn.leaky_relu(el[src] + er[dst], NEG_SLOPE)
            mx = jax.ops.segment_max(e, dst, num_segments=N)
            mx = jnp.where(jnp.isfinite(mx), mx, 0.0)
            ee = jnp.exp(e - mx[dst])
            denom = jax.ops.segment_sum(ee, dst, num_segments=N)
            alpha = ee / denom[dst]
            msg = feat[src] * alpha[:, :, None]
            rst = jax.ops.segment_sum(msg, dst, num_segments=N)
            rst = rst + bias.reshape(H, D)
            return jax.nn.elu(rst).reshape(N, HD)
        out = _gat(h, W_fc, attn_l, attn_r, bias, src, dst)
        z = out[:, None, :]
        w = (jnp.tanh(z @ sem_W1 + sem_b1) @ sem_W2).mean(0)
        beta = jax.nn.softmax(w, axis=0)
        return jnp.sum(beta * z, axis=1)

    def _L1_gnn_ref(x, W, edge_row, edge_col, edge_val):
        import jax, jax.numpy as jnp
        import numpy as np
        N = 100000
        E = 50000
        D_IN = 256
        D_OUT = 256
        support = jnp.einsum('nd,od->no', x.astype(jnp.float32), W.astype(jnp.float32))
        gathered = edge_val.astype(jnp.float32)[:, None] * support[edge_col]
        out = jax.ops.segment_sum(gathered, edge_row, num_segments=N)
        return out

    def _L2_gnn_ref(x, edge_index, lin_w, att, ln_w, ln_b):
        import jax, jax.numpy as jnp
        import numpy as np
        N_NODES = 50000
        N_EDGES = 12500
        IN_CH = 256
        HEADS = 8
        HEAD_DIM = 32
        NEG_SLOPE = 0.2
        LN_EPS = 1e-05
        SOFTMAX_EPS = 1e-16
        N = x.shape[0]
        src, dst = (edge_index[0], edge_index[1])
        xp = (x @ lin_w).reshape(N, HEADS, HEAD_DIM)
        att_i, att_j = (att[:, :HEAD_DIM], att[:, HEAD_DIM:])
        a_i = jnp.einsum('nhc,hc->nh', xp, att_i)
        a_j = jnp.einsum('nhc,hc->nh', xp, att_j)
        alpha = a_i[dst] + a_j[src]
        alpha = jnp.where(alpha >= 0, alpha, NEG_SLOPE * alpha)
        amax = jax.ops.segment_max(alpha, dst, num_segments=N)
        amax = jnp.where(jnp.isfinite(amax), amax, 0.0)
        ex = jnp.exp(alpha - amax[dst])
        denom = jax.ops.segment_sum(ex, dst, num_segments=N)
        alpha = ex / (denom[dst] + SOFTMAX_EPS)
        msg = xp[src] * alpha[:, :, None]
        out = jax.ops.segment_sum(msg, dst, num_segments=N)
        out = out.reshape(N, HEADS * HEAD_DIM)
        mu = out.mean(axis=-1, keepdims=True)
        var = ((out - mu) ** 2).mean(axis=-1, keepdims=True)
        out = (out - mu) * jax.lax.rsqrt(var + LN_EPS) * ln_w + ln_b
        out = jax.nn.elu(out)
        return out + x

    def _L3_gnn_ref(features, edge_src, edge_dst, edge_weight, W, b):
        import jax, jax.numpy as jnp
        import numpy as np
        N_NODES = 100000
        N_EDGES = 50000
        IN_FEATS = 256
        OUT_FEATS = 256
        msgs = features[edge_src] * edge_weight[:, None]
        agg = jax.ops.segment_sum(msgs, edge_dst, num_segments=N_NODES, indices_are_sorted=True)
        return jnp.einsum('ni,oi->no', agg, W) + b
    edge_index = jnp.stack([src, dst])
    x = _layernorm(x + _L0_gnn_ref(x, L0_gnn_W_fc, L0_gnn_attn_l, L0_gnn_attn_r, L0_gnn_bias, L0_gnn_sem_W1, L0_gnn_sem_b1, L0_gnn_sem_W2, src, dst), axis=-1)
    x = _layernorm(x + _L1_gnn_ref(x, L1_gnn_W, src, dst, edge_weight), axis=-1)
    x = _layernorm(x + _L2_gnn_ref(x, edge_index, L2_gnn_lin_w, L2_gnn_att, L2_gnn_ln_w, L2_gnn_ln_b), axis=-1)
    x = _layernorm(x + _L3_gnn_ref(x, src, dst, edge_weight, L3_gnn_W, L3_gnn_b), axis=-1)
    return x

_drawn_inputs = setup_inputs


def setup_inputs(seed=0):
    import zlib

    import numpy as np

    out = dict(_drawn_inputs(seed))
    spreads = {'L0_gnn_bias': (0.0, 0.1),
     'L0_gnn_sem_b1': (0.0, 0.1),
     'L2_gnn_ln_w': (1.0, 0.2),
     'L2_gnn_ln_b': (0.0, 0.1)}
    factors = {'L0_gnn_attn_l': 6.726, 'L0_gnn_attn_r': 8.0, 'L2_gnn_att': 5.087}
    for name, (base, spread) in spreads.items():
        noise = np.random.default_rng([zlib.crc32(name.encode()), seed]).standard_normal(out[name].shape)
        drawn = base * np.exp(spread * noise) if base else spread * noise
        out[name] = jnp.asarray(drawn.astype(out[name].dtype))
    for name, factor in factors.items():
        out[name] = (out[name] * factor).astype(out[name].dtype)
    return out
```

```python
from contextlib import ExitStack

import numpy as np

import concourse.bass as bass
from concourse import mybir

F32 = mybir.dt.float32
I32 = mybir.dt.int32
ALU = mybir.AluOpType
ACT = mybir.ActivationFunctionType
AX = mybir.AxisListType

N, E, F = 100000, 25000, 256
H, D = 8, 32
P = 128
KC = F // P
U = 4
GE = U * P
G = -(-E // GE)
EP = G * GE
T = EP // P
R = 16
NB = P * R
NF = N // NB
W = F + 1
DUMP = N + 8
NT = DUMP + P
FAR = float(1 << 20)
NONE = 65536.0
LOW = -1.0e30
LN_EPS = 1e-5
SOFTMAX_EPS = 1e-16


class Sems:

    def __init__(self, nc, ctx, tag):
        self.nc, self.ctx, self.tag, self.all = nc, ctx, tag, []

    def __call__(self, name):
        self.all.append(self.ctx.enter_context(self.nc.semaphore(f"{name}_{self.tag}")))
        return self.all[-1]

    def clear(self):
        for sem in self.all:
            self.nc.gpsimd.sem_clear(sem)
        self.nc.all_engine_barrier()


class Count:

    def __init__(self, sem, per):
        self.sem, self.per = sem, per

    def start(self, g):
        self.base, self.k = g * self.per, 0

    def up(self, instruction):
        instruction.then_inc(self.sem, 1)
        self.k += 1
        return self.base + self.k

    def end(self):
        assert self.k == self.per, (self.sem, self.k, self.per)


class Round:

    def __init__(self, g, b, n):
        self.g, self.b, self.n = g, b, n
        self.first = isinstance(g, int) and g == 0
        self.reused = not self.first


def rounds(eng, body):
    body(Round(0, 0, 0))
    turns = (G - 1) // 2 - 1
    with eng.Fori(0, turns) as i:
        body(Round(i * 2 + 1, 1, i))
        body(Round(i * 2 + 2, 0, i + 1))
    body(Round(G - 2, 1, turns))
    body(Round(G - 1, 0, turns + 1))


def before(r):
    return Round(r.g - 1, 1 - r.b, r.n - (1 - r.b))


LAST = Round(G - 1, (G - 1) % 2, (G - 1) // 2)


class Vec:

    def __init__(self, v, sem, per):
        self.v, self.c = v, Count(sem, per)

    def do(self, instruction):
        self.c.up(instruction)

    def wait(self):
        self.v.wait_ge(self.c.sem, self.c.base + self.c.k)

    def then(self, instruction):
        self.do(instruction)
        self.wait()


def block_rows(r):
    return N - NB if isinstance(r.g, int) and r.g == G - 1 else r.g * NB


def build(nc, x, pair_idx, dst_run, dst_cols, dst_next, w_cols, src_rev, src_rev_rows, dst_rev, dst_next_rev,
          w_rev, pos_rev, dump_col, ident_in, heads_in, later_in, w_fc, lin_w, w1t, w3t, attn_l, attn_r, att,
          bias_row, bias_cols, ln_w, ln_b, b3, out):
    node_table = nc.dram_tensor("node_table", [NT, W], F32, kind="Internal").ap()
    gat1_rows = nc.dram_tensor("gat1_rows", [EP, W], F32, kind="Internal").ap()
    gat2_rows = nc.dram_tensor("gat2_rows", [EP, W], F32, kind="Internal").ap()

    whole = ExitStack()
    with whole:
        def keep(name, shape, dt=F32):
            return whole.enter_context(nc.sbuf_tensor(name, shape, dt))

        ident = keep("ident", [P, P])
        heads = keep("heads", [H, KC, P])
        weights = {}
        for name in ("fc", "lin", "w1t", "w3t"):
            weights[name] = keep(name, [P, KC, F])
        att_src = {name: keep("att_src_" + name, [P, KC, H]) for name in ("fc", "lin")}
        att_dst = {name: keep("att_dst_" + name, [P, KC, H]) for name in ("fc", "lin")}
        biasT = keep("biasT", [P, KC])
        elu_bias = keep("elu_bias", [P, F])
        elu_lnb = keep("elu_lnb", [P, F])
        lnw_b = keep("lnw_b", [P, F])
        lnb_b = keep("lnb_b", [P, F])
        b3_b = keep("b3_b", [P, F])
        last_idx = keep("last_idx", [P, T], I32)
        run_end = keep("run_end", [P, T], I32)
        srcf_rev = keep("srcf_rev", [P, T])
        wrev = keep("wrev", [P, T])
        wcols = keep("wcols", [P, T])
        later = keep("later", [P, P])
        dump = keep("dump", [P, 1])

        setup(nc, locals())
        gat_phase(nc, locals(), "fc", 1)
        scatter_phase(nc, locals(), gat1_rows, node_table, "gat1")
        add_phase(nc, locals())
        gat_phase(nc, locals(), "lin", 2)
        scatter_phase(nc, locals(), gat2_rows, node_table, "gat2")
        last_phase(nc, locals())


def setup(nc, m):
    with ExitStack() as ctx:
        sb = lambda name, shape, dt=F32: ctx.enter_context(nc.sbuf_tensor(name, shape, dt))
        sem = Sems(nc, ctx, "setup")
        att_rows = sb("att_rows", [P, 2, F])
        att_row2 = sb("att_row2", [P, H, 2 * D])
        bias_b = sb("bias_b", [P, F])
        prod = sb("prod", [P, KC, F])
        neg = sb("neg", [P, 2, F])
        ex = sb("ex", [P, 2, F])
        ints = sb("ints", [P, 5, T], I32)
        eq = sb("eq", [P, T])
        cand = sb("cand", [P, T])
        pos = sb("pos", [P, T])
        run_min = sb("run_min", [P, T])
        row = sb("row", [1, P + 1])
        row_min = sb("row_min", [1, P])
        one = sb("one", [1, 1])
        after = sb("after", [P, 1])
        zeros = sb("zeros", [P, 2 * W])
        ps_row = ctx.enter_context(nc.psum_tensor("ps_row", [1, P], F32))
        ps_col = ctx.enter_context(nc.psum_tensor("ps_col", [P, 1], F32))
        loaded, chain, neg_done, ex_done = sem("loaded"), sem("chain0"), sem("neg_done"), sem("ex_done")
        col_ready, row_done, row_ready, col_done, zeroed = (
            sem("col_ready"), sem("row_done"), sem("row_ready"), sem("col_done"), sem("zeroed"))
        dump_clear = sem("dump_clear")
        loads = [
            (m["ident"][:, :], m["ident_in"]), (m["heads"][:, :, :], m["heads_in"]), (m["later"][:, :], m["later_in"]),
            (m["dump"][:, :], m["dump_col"]), (m["biasT"][:, :], m["bias_cols"]),
            (m["wrev"][:, :], m["w_rev"]), (m["wcols"][:, :], m["w_cols"]), (pos[:, :], m["pos_rev"]),
            (ints[:, 0, :], m["dst_cols"]), (ints[:, 1, :], m["dst_next"]), (ints[:, 2, :], m["dst_rev"]),
            (ints[:, 3, :], m["dst_next_rev"]), (ints[:, 4, :], m["src_rev"]),
            (att_rows[:, 0, :], m["attn_l"].partition_broadcast(P)),
            (att_rows[:, 1, :], m["attn_r"].partition_broadcast(P)),
            (att_row2[:, :, :].rearrange("p h c -> p (h c)"), m["att"].partition_broadcast(P)),
            (bias_b[:, :], m["bias_row"].partition_broadcast(P)),
            (m["lnw_b"][:, :], m["ln_w"].partition_broadcast(P)),
            (m["lnb_b"][:, :], m["ln_b"].partition_broadcast(P)),
            (m["b3_b"][:, :], m["b3"].partition_broadcast(P)),
        ] + [(m["weights"][k][:, :, :], m[d].rearrange("(c p) n -> p c n", p=P))
             for k, d in (("fc", "w_fc"), ("lin", "lin_w"), ("w1t", "w1t"), ("w3t", "w3t"))]

        with nc.Block() as block:
            @block.sync
            def _(sp):
                for dst, src in loads:
                    sp.dma_start(dst, src).then_inc(loaded, 16)
                sp.wait_ge(zeroed, 1)
                sp.dma_start(m["node_table"][N:NT, :], zeros[0:NT - N, 0:W] if NT - N <= P else
                             zeros[0:(NT - N) // 2, :].rearrange("p (a w) -> p a w", a=2)).then_inc(dump_clear, 16)
                sp.wait_ge(dump_clear, 16)

            @block.scalar
            def _(act):
                act.wait_ge(loaded, 16 * len(loads))
                nc.scalar.activation(neg[:, 0, :], bias_b[:, :], ACT.Relu, scale=-1.0).then_inc(neg_done, 1)
                nc.scalar.activation(neg[:, 1, :], m["lnb_b"][:, :], ACT.Relu, scale=-1.0).then_inc(neg_done, 1)
                act.wait_ge(neg_done, 2)
                nc.scalar.activation(ex[:, :, :], neg[:, :, :], ACT.Exp, scale=-1.0).then_inc(ex_done, 1)

            @block.vector
            def _(v):
                c = Vec(v, chain, 0)
                c.c.start(0)
                nc.vector.memset(zeros[:, :], 0.0).then_inc(zeroed, 1)
                c.do(nc.vector.memset(row[0:1, 0:1], NONE))
                c.then(nc.vector.memset(one[:, :], 1.0))
                v.wait_ge(loaded, 16 * len(loads))
                c.then(nc.vector.tensor_tensor(eq[:, :], ints[:, 2, :], ints[:, 3, :], ALU.is_equal))
                c.then(nc.vector.scalar_tensor_tensor(out=cand[:, :], in0=eq[:, :], scalar=NONE, in1=pos[:, :],
                                                      op0=ALU.mult, op1=ALU.add))
                nc.vector.tensor_tensor_scan(run_min[:, :], cand[:, :], cand[:, :], NONE, ALU.min,
                                             ALU.min).then_inc(col_ready, 1)
                for name, parts in (("fc", (att_rows[:, 0, :], att_rows[:, 1, :])),
                                    ("lin", (att_row2[:, :, D:2 * D], att_row2[:, :, 0:D]))):
                    for goal, part in zip((m["att_src"][name], m["att_dst"][name]), parts):
                        for k in range(KC):
                            a, w = prod[:, k, :], m["weights"][name][:, k, :]
                            if name == "lin":
                                a, w = (t.rearrange("p (h c) -> p h c", h=H) for t in (a, w))
                            c.then(nc.vector.tensor_tensor(a, w, part, ALU.mult))
                            c.then(nc.vector.tensor_reduce(goal[:, k, :], prod[:, k, :].rearrange("p (h c) -> p h c", h=H),
                                                           AX.X, ALU.add))
                v.wait_ge(ex_done, 1)
                for k, (goal, b) in enumerate(((m["elu_bias"], bias_b), (m["elu_lnb"], m["lnb_b"]))):
                    c.do(nc.vector.scalar_tensor_tensor(out=goal[:, :], in0=ex[:, k, :], scalar=-1.0, in1=b[:, :],
                                                        op0=ALU.add, op1=ALU.max))
                c.then(nc.vector.tensor_tensor(eq[:, :], ints[:, 0, :], ints[:, 1, :], ALU.is_equal))
                c.then(nc.vector.scalar_tensor_tensor(out=cand[:, :], in0=eq[:, :], scalar=FAR, in1=ints[:, 0, :],
                                                      op0=ALU.mult, op1=ALU.add))
                c.do(nc.vector.tensor_copy(m["last_idx"][:, :], cand[:, :]))
                c.do(nc.vector.tensor_copy(m["srcf_rev"][:, :], ints[:, 4, :]))
                v.wait_ge(row_done, 1)
                c.then(nc.vector.tensor_copy(row[0:1, 1:P + 1], ps_row[0:1, :]))
                nc.vector.tensor_tensor_scan(row_min[0:1, :], row[0:1, 0:P], row[0:1, 0:P], NONE, ALU.min,
                                             ALU.min).then_inc(row_ready, 1)
                v.wait_ge(col_done, 1)
                c.then(nc.vector.tensor_copy(after[:, :], ps_col[:, :]))
                c.then(nc.vector.tensor_scalar(cand[:, :], run_min[:, :], after[:, 0:1], None, ALU.min))
                c.then(nc.vector.tensor_copy(m["run_end"][:, :], cand[:, :]))

            @block.tensor
            def _(pe):
                pe.wait_ge(loaded, 16 * len(loads))
                pe.wait_ge(col_ready, 1)
                nc.tensor.matmul(ps_row[0:1, :], run_min[:, T - 1:T], m["ident"][:, :], start=True,
                                 stop=True).then_inc(row_done, 1)
                pe.wait_ge(row_ready, 1)
                nc.tensor.matmul(ps_col[:, 0:1], row_min[0:1, :], one[0:1, 0:1], start=True, stop=True).then_inc(col_done, 1)
        sem.clear()


def norm_scalars(c, v, nc, st, w, n, lnx, rs, scale_ready, act_done, act_value):
    me, cve, mo, cvo = st[:, :, 1], st[:, :, 2], st[:, :, 4], st[:, :, 5]
    c.do(nc.vector.tensor_tensor(w[:, 0, 0:n], me, mo, ALU.subtract))
    c.do(nc.vector.tensor_tensor(w[:, 1, 0:n], cve, cvo, ALU.add))
    c.then(nc.vector.tensor_tensor(w[:, 4, 0:n], me, mo, ALU.add))
    c.do(nc.vector.tensor_scalar(w[:, 4, 0:n], w[:, 4, 0:n], 0.5, None, ALU.mult))
    c.then(nc.vector.tensor_tensor(w[:, 2, 0:n], w[:, 0, 0:n], w[:, 0, 0:n], ALU.mult))
    c.then(nc.vector.scalar_tensor_tensor(out=w[:, 2, 0:n], in0=w[:, 2, 0:n], scalar=F / 4.0, in1=w[:, 1, 0:n],
                                          op0=ALU.mult, op1=ALU.add))
    nc.vector.tensor_scalar(lnx[:, 0, 0:n], w[:, 2, 0:n], 1.0 / F, LN_EPS, ALU.mult,
                            ALU.add).then_inc(scale_ready, 1)
    v.wait_ge(act_done, act_value)
    c.then(nc.vector.tensor_tensor(w[:, 0, 0:n], lnx[:, 2, 0:n], lnx[:, 2, 0:n], ALU.mult))
    c.then(nc.vector.tensor_tensor(w[:, 1, 0:n], w[:, 0, 0:n], lnx[:, 0, 0:n], ALU.mult))
    c.then(nc.vector.tensor_scalar(w[:, 2, 0:n], w[:, 1, 0:n], -0.5, 1.5, ALU.mult, ALU.add))
    c.then(nc.vector.tensor_tensor(rs[:, 0, 0:n], lnx[:, 2, 0:n], w[:, 2, 0:n], ALU.mult))


def minus_mean(nc, w, rs, n):
    return nc.vector.scalar_tensor_tensor(out=rs[:, 1, 0:n], in0=w[:, 4, 0:n], scalar=-1.0, in1=rs[:, 0, 0:n],
                                          op0=ALU.mult, op1=ALU.mult)


def root(nc, act, lnx, n, asked, value, halfway, done):
    act.wait_ge(asked, value)
    nc.scalar.activation(lnx[:, 1, 0:n], lnx[:, 0, 0:n], ACT.Ln).then_inc(halfway, 1)
    act.wait_ge(halfway, value)
    nc.scalar.activation(lnx[:, 2, 0:n], lnx[:, 1, 0:n], ACT.Exp, scale=-0.5).then_inc(done, 1)


NORM_STEPS = 10


def gat_phase(nc, m, name, layer):
    two = layer == 2
    RW = W if two else F
    ends = m["node_table"][0:N, :] if two else m["x"]
    kept = m["gat2_rows"] if two else m["gat1_rows"]
    ident, heads, wgt = m["ident"], m["heads"], m["weights"][name]
    a_src, a_dst = m["att_src"][name], m["att_dst"][name]
    with ExitStack() as ctx:
        sb = lambda n, shape, dt=F32: ctx.enter_context(nc.sbuf_tensor(f"{n}_{layer}", shape, dt))
        pb = lambda n, shape: ctx.enter_context(nc.psum_tensor(f"{n}_{layer}", shape, F32))
        sem = Sems(nc, ctx, layer)
        two_of = lambda n, shape, dt=F32: [sb(f"{n}{i}", shape, dt) for i in range(2)]

        idx = two_of("idx", [P, 2 * U], I32)
        runs = two_of("runs", [H, 2, GE], I32)
        raw = two_of("raw", [P, 2 * U, RW])
        rows = two_of("rows", [P, 2 * U, F]) if two else raw
        srcT = two_of("srcT", [P, KC, GE])
        dstT = two_of("dstT", [P, KC, GE])
        logit = sb("logit", [H, GE])
        leaky = sb("leaky", [H, GE])
        same = sb("same", [H, GE])
        pen = sb("pen", [H, GE])
        top = sb("top", [H, GE + 1])
        diff = sb("diff", [H, 2, GE])
        probs = sb("probs", [H, 2, GE])
        den = sb("den", [H, GE + 1])
        rden = sb("rden", [H, GE])
        pcopy = sb("pcopy", [P, KC, GE])
        msg = sb("msg", [P, KC, GE])
        agg = sb("agg", [P, KC, GE])
        carry = sb("carry", [P, KC])
        yT = sb("yT", [P, KC, GE])
        eT = sb("eT", [P, KC, GE])
        yrow = sb("yrow", [P, U, F])
        y2row = sb("y2row", [P, U, F])
        erow = sb("erow", [P, U, F])
        kept_rows = two_of("kept_rows", [P, U, W])
        stF, stT, stT2 = sb("stF", [P, 2 * U, 6]), sb("stT", [P, U, 6]), sb("stT2", [P, U, 6])
        wk = sb("wk", [P, 5, 2 * U])
        lnx = sb("lnx", [P, 3, 2 * U])
        rs = [sb(f"rs{i}", [P, 2, 2 * U]) for i in range(3)]
        xb = two_of("xb", [P, R, RW])
        ob = two_of("ob", [P, R, W if not two else F])
        stD = sb("stD", [P, R, 6])
        wkD, lnxD, rsD = sb("wkD", [P, 5, R]), sb("lnxD", [P, 3, R]), sb("rsD", [P, 2, R])

        turn = pb("turn", [P, KC, GE])
        ps_log = turn[0:H, 0, :]
        feat = pb("feat", [P, KC, GE])
        bcast = [pb(f"bcast{c}", [P, GE]) for c in range(KC)]
        back = pb("back", [P, U, F])

        idx_in, runs_in = [sem(f"idx_in{i}") for i in range(2)], [sem(f"runs_in{i}") for i in range(2)]
        got = [sem(f"got{i}") for i in range(2)]
        kept_out = [sem(f"kept_out{i}") for i in range(2)]
        x_in, o_out = [sem(f"x_in{i}") for i in range(2)], [sem(f"o_out{i}") for i in range(2)]
        marked, released = sem("marked"), sem("released")
        rows_asked, rows_half, rows_root, rows_scaled, rows_normed = (
            sem("rows_asked"), sem("rows_half"), sem("rows_root"), sem("rows_scaled"), sem("rows_normed"))
        turned, copied, logits_done, logits_copied, feats_done = (
            sem("turned"), sem("copied"), sem("logits_done"), sem("logits_copied"), sem("feats_done"))
        leaky_done, diffs_ready, exps_ready, rden_ready = (
            sem("leaky_done"), sem("diffs_ready"), sem("exps_ready"), sem("rden_ready"))
        spread, p_copied, msgs_done, scans_done, scaled, biased, negs, exps, y_ready = (
            sem("spread"), sem("p_copied"), sem("msgs_done"), sem("scans_done"), sem("scaled"), sem("biased"),
            sem("negs"), sem("exps"), sem("y_ready"))
        runs_read = sem("runs_read")
        turned_back, back_read, t_asked, t_half, t_root, t_scaled = (
            sem("turned_back"), sem("back_read"), sem("t_asked"), sem("t_half"), sem("t_root"), sem("t_scaled"))
        o_normed, affine, o_neg, o_exp, u_asked, u_half, u_root, u_scaled = (
            sem("o_normed"), sem("affine"), sem("o_neg"), sem("o_exp"), sem("u_asked"), sem("u_half"), sem("u_root"), sem("u_scaled"))
        d_asked, d_half, d_root, d_scaled, d_normed = (
            sem("d_asked"), sem("d_half"), sem("d_root"), sem("d_scaled"), sem("d_normed"))
        chF, chM, chT, chD = sem("chF"), sem("chM"), sem("chT"), sem("chD")

        with nc.Block() as block:
            @block.gpsimd
            def _(pool):
                bound = pool.to_reg(N - 1)

                def gather(r):
                    pool.wait_ge(idx_in[r.b], (r.n + 1) * 16)
                    if r.reused:
                        if two:
                            pool.wait_ge(rows_normed, r.g - 1)
                        else:
                            pool.wait_ge(turned, (r.g - 1) * 2)
                    pool.sem_inc(released, 1)
                    for j in range(2 * U):
                        nc.gpsimd.indirect_dma_start(
                            raw[r.b][:, j, :], None, ends, bass.IndirectOffsetOnAxis(ap=idx[r.b][:, j:j + 1], axis=0),
                            bounds_check=bound, oob_is_err=False).then_inc(got[r.b], 16)
                rounds(pool, gather)

            @block.sync
            def _(sp):
                def load(r):
                    if r.reused:
                        sp.wait_ge(got[r.b], r.n * 2 * U * 16)
                        sp.wait_ge(runs_read, r.g - 1)
                    sp.dma_start(idx[r.b][:, :], m["pair_idx"][bass.ds(r.g, 1), :, :].rearrange("a p n -> (a p) n")
                                 ).then_inc(idx_in[r.b], 16)
                    for k in range(2):
                        sp.dma_start(runs[r.b][:, k, :], m["dst_run"][0:1, bass.ds(r.g * GE + k, GE)].partition_broadcast(H)
                                     ).then_inc(runs_in[r.b], 16)
                    if r.reused:
                        sp.wait_ge(d_normed, r.g - 1)
                    src = m["node_table"] if two else m["x"]
                    sp.dma_start(xb[r.b][:, :, :], src[bass.ds(block_rows(r), NB), :].rearrange("(p r) n -> p r n", p=P)
                                 ).then_inc(x_in[r.b], 16)

                def store(r):
                    dst = m["out"] if two else m["node_table"]
                    sp.wait_ge(d_normed, r.g + 1)
                    if isinstance(r.g, int) and r.g == G - 1:
                        sp.wait_ge(o_out[1 - r.b], r.n * 16)
                    sp.dma_start(dst[bass.ds(block_rows(r), NB), :].rearrange("(p r) n -> p r n", p=P), ob[r.b][:, :, :]
                                 ).then_inc(o_out[r.b], 16)

                def store_rows(r):
                    sp.wait_ge(o_normed if two else back_read, r.g + 1)
                    sp.dma_start(kept[bass.ds(r.g * GE, GE), :].rearrange("(u p) n -> p u n", p=P), kept_rows[r.b][:, :, :]
                                 ).then_inc(kept_out[r.b], 16)

                sp.wait_ge(marked, 1)

                def body(r):
                    load(r)
                    if r.reused:
                        store(before(r))
                        store_rows(before(r))
                rounds(sp, body)
                store(LAST)
                store_rows(LAST)
                for b in range(2):
                    uses = (G + 1 - b) // 2
                    sp.wait_ge(kept_out[b], uses * 16)
                    sp.wait_ge(o_out[b], uses * 16)

            @block.tensor
            def _(pe):
                def front(r):
                    if two:
                        pe.wait_ge(rows_normed, r.g + 1)
                    else:
                        pe.wait_ge(got[r.b], (r.n + 1) * 2 * U * 16)
                    for side in range(2):
                        if side == 0:
                            pe.wait_ge(logits_copied, r.g * 1)
                        else:
                            pe.wait_ge(copied, r.g * 2 + 1)
                        for c in range(KC):
                            for u in range(U):
                                t = nc.tensor.transpose(turn[:, c, u * P:(u + 1) * P],
                                                        rows[r.b][:, side * U + u, c * P:(c + 1) * P], ident[:, :])
                        t.then_inc(turned, 1)
                    pe.wait_ge(copied, r.g * 2 + 2)
                    for k in range(2 * KC):
                        s = k < KC
                        t = nc.tensor.matmul(ps_log, (a_src if s else a_dst)[:, k % KC, :],
                                             (srcT if s else dstT)[r.b][:, k % KC, :], start=(k == 0), stop=(k == 2 * KC - 1))
                    t.then_inc(logits_done, 1)
                    pe.wait_ge(msgs_done, r.g * 2)
                    for c in range(KC):
                        for k in range(KC):
                            t = nc.tensor.matmul(feat[:, c, :], wgt[:, k, c * P:(c + 1) * P], srcT[r.b][:, k, :],
                                                 start=(k == 0), stop=(k == KC - 1))
                    t.then_inc(feats_done, 1)

                def middle(r):
                    pe.wait_ge(exps_ready, r.g + 1)
                    for c in range(KC):
                        if not r.first:
                            pe.wait_ge(scaled, r.g * 2 - 1 + c)
                        nc.tensor.matmul(bcast[c][:, :], heads[:, c, :], probs[:, 1, :], start=True, stop=True).then_inc(spread, 1)
                    for c in range(KC):
                        pe.wait_ge(p_copied, r.g * 2 + c + 1)
                        nc.tensor.matmul(bcast[c][:, :], heads[:, c, :], probs[:, 0, :], start=True, stop=True).then_inc(spread, 1)
                    pe.wait_ge(rden_ready, r.g + 1)
                    for c in range(KC):
                        pe.wait_ge(scans_done, r.g * 2 + c + 1)
                        nc.tensor.matmul(bcast[c][:, :], heads[:, c, :], rden[:, :], start=True, stop=True).then_inc(spread, 1)

                def tail(r):
                    if two:
                        pe.wait_ge(scaled, r.g * 2 + 2)
                    else:
                        pe.wait_ge(y_ready, r.g + 1)
                    pe.wait_ge(back_read, r.g * 1)
                    for u in range(U):
                        for c in range(KC):
                            t = nc.tensor.transpose(back[:, u, c * P:(c + 1) * P], yT[:, c, u * P:(u + 1) * P], ident[:, :])
                    t.then_inc(turned_back, 1)

                def body(r):
                    if r.reused:
                        tail(before(r))
                    front(r)
                    middle(r)
                rounds(pe, body)
                tail(LAST)

            @block.scalar
            def _(act):
                def front(r):
                    if two:
                        root(nc, act, lnx, 2 * U, rows_asked, r.g + 1, rows_half, rows_root)
                        act.wait_ge(rows_scaled, r.g + 1)
                        if r.reused:
                            act.wait_ge(turned, (r.g - 1) * 2)
                        for j in range(2 * U):
                            t = nc.scalar.activation(rows[r.b][:, j, :], raw[r.b][:, j, 0:F], ACT.Identity,
                                                     bias=rs[0][:, 1, j:j + 1], scale=rs[0][:, 0, j:j + 1])
                        t.then_inc(rows_normed, 1)
                    act.wait_ge(turned, r.g * 2 + 1)
                    if r.reused:
                        act.wait_ge(feats_done, (r.g - 1))
                    nc.scalar.activation(srcT[r.b][:, :, :], turn[:, :, :], ACT.Copy).then_inc(copied, 1)
                    act.wait_ge(turned, r.g * 2 + 2)
                    if r.reused and not two:
                        act.wait_ge(y_ready, r.g - 1)
                    nc.scalar.activation(dstT[r.b][:, :, :], turn[:, :, :], ACT.Copy).then_inc(copied, 1)

                def middle(r):
                    act.wait_ge(logits_done, r.g + 1)
                    act.wait_ge(leaky_done, r.g * 1)
                    nc.scalar.activation(logit[:, :], ps_log, ACT.Copy).then_inc(logits_copied, 1)
                    act.wait_ge(diffs_ready, r.g + 1)
                    if r.reused:
                        act.wait_ge(spread, r.g * 6)
                        act.wait_ge(rden_ready, r.g)
                    nc.scalar.activation(probs[:, :, :], diff[:, :, :], ACT.Exp).then_inc(exps_ready, 1)
                    for c in range(KC):
                        act.wait_ge(spread, r.g * 6 + c + 1)
                        act.wait_ge(msgs_done, r.g * 2)
                        nc.scalar.activation(pcopy[:, c, :], bcast[c][:, :], ACT.Copy).then_inc(p_copied, 1)
                    act.wait_ge(d_scaled, r.g + 1)
                    if r.reused:
                        act.wait_ge(o_out[r.b], r.n * 16)
                    for j in range(R):
                        t = nc.scalar.activation(ob[r.b][:, j, 0:F], xb[r.b][:, j, 0:F], ACT.Identity,
                                                 bias=rsD[:, 1, j:j + 1], scale=rsD[:, 0, j:j + 1])
                    t.then_inc(d_normed, 1)
                    if not two:
                        for c in range(KC):
                            act.wait_ge(scaled, r.g * 2 + c + 1)
                            act.wait_ge(y_ready, r.g * 1)
                            nc.scalar.activation(msg[:, c, :], agg[:, c, :], ACT.Identity,
                                                 bias=m["biasT"][:, c:c + 1]).then_inc(biased, 1)
                        act.wait_ge(biased, r.g * 2 + 2)
                        nc.scalar.activation(eT[:, :, :], msg[:, :, :], ACT.Relu, scale=-1.0).then_inc(negs, 1)
                        act.wait_ge(negs, r.g + 1)
                        nc.scalar.activation(eT[:, :, :], eT[:, :, :], ACT.Exp, scale=-1.0).then_inc(exps, 1)

                def tail(r):
                    root(nc, act, lnx, U, t_asked, r.g + 1, t_half, t_root)
                    act.wait_ge(t_scaled, r.g + 1)
                    if not two:
                        if not r.first:
                            act.wait_ge(kept_out[r.b], r.n * 16)
                        goal = kept_rows[r.b]
                    else:
                        goal = yrow
                    for u in range(U):
                        t = nc.scalar.activation(goal[:, u, 0:F], back[:, u, :], ACT.Identity,
                                                 bias=rs[1][:, 1, u:u + 1], scale=rs[1][:, 0, u:u + 1])
                    t.then_inc(back_read, 1)
                    if two:
                        act.wait_ge(affine, r.g + 1)
                        nc.scalar.activation(erow[:, :, :], yrow[:, :, :], ACT.Relu, scale=-1.0).then_inc(o_neg, 1)
                        act.wait_ge(o_neg, r.g + 1)
                        nc.scalar.activation(erow[:, :, :], erow[:, :, :], ACT.Exp, scale=-1.0).then_inc(o_exp, 1)
                        root(nc, act, lnx, U, u_asked, r.g + 1, u_half, u_root)
                        act.wait_ge(u_scaled, r.g + 1)
                        if not r.first:
                            act.wait_ge(kept_out[r.b], r.n * 16)
                        for u in range(U):
                            t = nc.scalar.activation(kept_rows[r.b][:, u, 0:F], y2row[:, u, :], ACT.Identity,
                                                     bias=rs[2][:, 1, u:u + 1], scale=rs[2][:, 0, u:u + 1])
                        t.then_inc(o_normed, 1)

                def dense(r):
                    norms = 3 if two else 1
                    for k in range(norms):
                        root(nc, act, lnxD, R, d_asked, r.g * norms + k + 1, d_half, d_root)

                def body(r):
                    if r.reused:
                        tail(before(r))
                    front(r)
                    dense(r)
                    middle(r)
                rounds(act, body)
                tail(LAST)

            @block.vector
            def _(v):
                cF, cM, cT, cD = (Vec(v, s, n) for s, n in (
                    (chF, 2 * U + NORM_STEPS), (chM, 10),
                    (chT, 2 * (U + NORM_STEPS) + 3 if two else U + NORM_STEPS),
                    (chD, 3 * (R + NORM_STEPS) + 2 * R + 1 if two else R + NORM_STEPS + 1)))
                MARK = 1.0 if two else 0.0
                if not two:
                    for b in range(2):
                        nc.vector.memset(ob[b][:, :, F:W], 0.0)
                for b in range(2):
                    nc.vector.memset(kept_rows[b][:, :, F:W], MARK)
                nc.vector.memset(carry[:, :], 0.0)
                nc.vector.memset(den[:, GE:GE + 1], 0.0)
                nc.vector.memset(top[:, GE:GE + 1], 0.0).then_inc(marked, 1)
                v.wait_ge(marked, 1)

                def front(r):
                    cF.c.start(r.g)
                    v.wait_ge(got[r.b], (r.n + 1) * 2 * U * 16)
                    for j in range(2 * U):
                        cF.do(nc.vector.bn_stats(stF[:, j, :], raw[r.b][:, j, 0:F]))
                    cF.wait()
                    v.wait_ge(rows_normed, r.g * 1)
                    norm_scalars(cF, v, nc, stF, wk, 2 * U, lnx, rs[0], rows_asked, rows_root, r.g + 1)
                    minus_mean(nc, wk, rs[0], 2 * U).then_inc(rows_scaled, 1)
                    v.wait_ge(rows_scaled, r.g + 1)
                    cF.c.end()

                def dense(r):
                    cD.c.start(r.g)
                    norms = 3 if two else 1
                    x = xb[r.b]
                    v.wait_ge(x_in[r.b], (r.n + 1) * 16)
                    if not two:
                        cD.then(nc.vector.tensor_tensor(x[:, :, :], x[:, :, :],
                                                        m["elu_bias"][:, :].unsqueeze(1).to_broadcast([P, R, F]), ALU.add))
                    for k in range(norms):
                        for j in range(R):
                            cD.do(nc.vector.bn_stats(stD[:, j, :], x[:, j, 0:F]))
                        cD.wait()
                        if k == norms - 1:
                            v.wait_ge(d_normed, r.g * 1)
                        norm_scalars(cD, v, nc, stD, wkD, R, lnxD, rsD, d_asked, d_root, r.g * norms + k + 1)
                        if k == norms - 1:
                            minus_mean(nc, wkD, rsD, R).then_inc(d_scaled, 1)
                            v.wait_ge(d_scaled, r.g + 1)
                        else:
                            if k == 0:
                                cD.then(nc.vector.tensor_scalar(rsD[:, 0, :], rsD[:, 0, :], 2.0, None, ALU.mult))
                            plus = m["elu_lnb"] if k == 0 else m["b3_b"]
                            for j in range(R):
                                cD.do(nc.vector.scalar_tensor_tensor(out=x[:, j, 0:F], in0=x[:, j, 0:F], scalar=rsD[:, 0, j:j + 1],
                                                                     in1=plus[:, :], op0=ALU.mult, op1=ALU.add))
                            cD.wait()
                    cD.c.end()

                def middle(r):
                    cM.c.start(r.g)
                    v.wait_ge(runs_in[r.b], (r.n + 1) * 32)
                    nc.vector.tensor_tensor(same[:, :], runs[r.b][:, 0, :], runs[r.b][:, 1, :],
                                            ALU.is_equal).then_inc(runs_read, 1)
                    v.wait_ge(runs_read, r.g + 1)
                    cM.do(nc.vector.tensor_scalar(pen[:, :], same[:, :], -LOW, LOW, ALU.mult, ALU.add))
                    cM.do(nc.vector.tensor_copy(top[:, 0:1], top[:, GE:GE + 1]))
                    cM.do(nc.vector.tensor_copy(den[:, 0:1], den[:, GE:GE + 1]))
                    v.wait_ge(logits_copied, r.g + 1)
                    nc.vector.scalar_tensor_tensor(out=leaky[:, :], in0=logit[:, :], scalar=0.2, in1=logit[:, :],
                                                   op0=ALU.mult, op1=ALU.max).then_inc(leaky_done, 1)
                    v.wait_ge(leaky_done, r.g + 1)
                    cM.wait()
                    cM.then(nc.vector.tensor_tensor_scan(top[:, 1:GE + 1], pen[:, :], leaky[:, :], top[:, 0:1], ALU.add, ALU.max))
                    cM.do(nc.vector.tensor_tensor(diff[:, 1, :], leaky[:, :], top[:, 1:GE + 1], ALU.subtract))
                    cM.then(nc.vector.tensor_tensor(pen[:, :], pen[:, :], top[:, 0:GE], ALU.add))
                    nc.vector.tensor_tensor(diff[:, 0, :], pen[:, :], top[:, 1:GE + 1], ALU.subtract).then_inc(diffs_ready, 1)
                    v.wait_ge(diffs_ready, r.g + 1)
                    v.wait_ge(exps_ready, r.g + 1)
                    cM.then(nc.vector.tensor_tensor_scan(den[:, 1:GE + 1], probs[:, 0, :], probs[:, 1, :], den[:, 0:1],
                                                         ALU.mult, ALU.add))
                    v.wait_ge(spread, r.g * 6)
                    if two:
                        cM.then(nc.vector.tensor_scalar(rden[:, :], den[:, 1:GE + 1], SOFTMAX_EPS, None, ALU.add))
                    nc.vector.reciprocal(rden[:, :], rden[:, :] if two else den[:, 1:GE + 1]).then_inc(rden_ready, 1)
                    v.wait_ge(feats_done, r.g + 1)
                    for c in range(KC):
                        v.wait_ge(p_copied, r.g * 2 + c + 1)
                        nc.vector.tensor_tensor(msg[:, c, :], feat[:, c, :], pcopy[:, c, :], ALU.mult).then_inc(msgs_done, 1)
                    for c in range(KC):
                        v.wait_ge(spread, r.g * 6 + 3 + c)
                        v.wait_ge(msgs_done, r.g * 2 + c + 1)
                        nc.vector.tensor_tensor_scan(agg[:, c, :], bcast[c][:, :], msg[:, c, :], carry[:, c:c + 1],
                                                     ALU.mult, ALU.add).then_inc(scans_done, 1)
                    for c in range(KC):
                        v.wait_ge(scans_done, r.g * 2 + c + 1)
                        cM.do(nc.vector.tensor_copy(carry[:, c:c + 1], agg[:, c, GE - 1:GE]))
                    cM.wait()
                    v.wait_ge(turned_back, r.g * 1)
                    for c in range(KC):
                        v.wait_ge(spread, r.g * 6 + 5 + c)
                        nc.vector.tensor_tensor((yT if two else agg)[:, c, :], agg[:, c, :], bcast[c][:, :],
                                                ALU.mult).then_inc(scaled, 1)
                    if not two:
                        v.wait_ge(exps, r.g + 1)
                        cM.then(nc.vector.scalar_tensor_tensor(out=yT[:, :, :], in0=eT[:, :, :], scalar=-1.0, in1=msg[:, :, :],
                                                               op0=ALU.add, op1=ALU.max))
                        nc.vector.tensor_tensor(yT[:, :, :], yT[:, :, :], dstT[r.b][:, :, :], ALU.add).then_inc(y_ready, 1)
                    cM.c.end()

                def tail(r):
                    cT.c.start(r.g)
                    v.wait_ge(turned_back, r.g + 1)
                    for u in range(U):
                        cT.do(nc.vector.bn_stats(stT[:, u, :], back[:, u, :]))
                    cT.wait()
                    v.wait_ge(back_read, r.g * 1)
                    norm_scalars(cT, v, nc, stT, wk, U, lnx, rs[1], t_asked, t_root, r.g + 1)
                    minus_mean(nc, wk, rs[1], U).then_inc(t_scaled, 1)
                    v.wait_ge(t_scaled, r.g + 1)
                    if two:
                        v.wait_ge(back_read, r.g + 1)
                        row_of = lambda t: t[:, :].unsqueeze(1).to_broadcast([P, U, F])
                        cT.then(nc.vector.tensor_tensor(yrow[:, :, :], yrow[:, :, :], row_of(m["lnw_b"]), ALU.mult))
                        nc.vector.tensor_tensor(yrow[:, :, :], yrow[:, :, :], row_of(m["lnb_b"]), ALU.add).then_inc(affine, 1)
                        v.wait_ge(o_exp, r.g + 1)
                        v.wait_ge(affine, r.g + 1)
                        cT.then(nc.vector.scalar_tensor_tensor(out=yrow[:, :, :], in0=erow[:, :, :], scalar=-1.0,
                                                               in1=yrow[:, :, :], op0=ALU.add, op1=ALU.max))
                        v.wait_ge(o_normed, r.g * 1)
                        cT.then(nc.vector.scalar_tensor_tensor(out=y2row[:, :, :], in0=rows[r.b][:, U:2 * U, :], scalar=2.0,
                                                               in1=yrow[:, :, :], op0=ALU.mult, op1=ALU.add))
                        for u in range(U):
                            cT.do(nc.vector.bn_stats(stT[:, u, :], y2row[:, u, :]))
                        cT.wait()
                        norm_scalars(cT, v, nc, stT, wk, U, lnx, rs[2], u_asked, u_root, r.g + 1)
                        minus_mean(nc, wk, rs[2], U).then_inc(u_scaled, 1)
                        v.wait_ge(u_scaled, r.g + 1)
                    cT.c.end()

                def body(r):
                    if r.reused:
                        tail(before(r))
                    if two:
                        front(r)
                    dense(r)
                    middle(r)
                rounds(v, body)
                tail(LAST)
        sem.clear()


def scatter_phase(nc, m, kept, table, tag):
    with ExitStack() as ctx:
        sb = lambda n, shape, dt=F32: ctx.enter_context(nc.sbuf_tensor(f"{n}_{tag}", shape, dt))
        sem = Sems(nc, ctx, tag)
        rows = [sb(f"rows{i}", [P, U, W]) for i in range(2)]
        idx = [sb(f"idx{i}", [P, U], I32) for i in range(2)]
        rows_in = [sem(f"rows_in{i}") for i in range(2)]
        idx_ready, released, written = sem("idx_ready"), sem("released"), [sem(f"written{i}") for i in range(2)]
        with nc.Block() as block:
            @block.sync
            def _(sp):
                def load(r):
                    if r.reused:
                        sp.wait_ge(written[r.b], r.n * U * 16)
                    sp.dma_start(rows[r.b][:, :, :], kept[bass.ds(r.g * GE, GE), :].rearrange("(u p) n -> p u n", p=P)
                                 ).then_inc(rows_in[r.b], 16)
                rounds(sp, load)

            @block.vector
            def _(v):
                def pick(r):
                    if r.reused:
                        v.wait_ge(written[r.b], r.n * U * 16)
                    nc.vector.tensor_copy(idx[r.b][:, :], m["last_idx"][:, bass.ds(r.g * U, U)]).then_inc(idx_ready, 1)
                rounds(v, pick)

            @block.gpsimd
            def _(pool):
                bound = pool.to_reg(N - 1)

                def scatter(r):
                    pool.wait_ge(idx_ready, r.g + 1)
                    pool.wait_ge(rows_in[r.b], (r.n + 1) * 16)
                    if r.reused:
                        pool.wait_ge(written[r.b], r.n * U * 16)
                    pool.sem_inc(released, 1)
                    for u in range(U):
                        nc.gpsimd.indirect_dma_start(
                            table[0:N, :], bass.IndirectOffsetOnAxis(ap=idx[r.b][:, u:u + 1], axis=0), rows[r.b][:, u, :], None,
                            bounds_check=bound, oob_is_err=False).then_inc(written[r.b], 16)
                rounds(pool, scatter)
                for b in range(2):
                    pool.wait_ge(written[b], (G + 1 - b) // 2 * U * 16)
        sem.clear()


def add_phase(nc, m):
    ident, w1t = m["ident"], m["weights"]["w1t"]
    with ExitStack() as ctx:
        sb = lambda n, shape, dt=F32: ctx.enter_context(nc.sbuf_tensor(f"{n}_add", shape, dt))
        pb = lambda n, shape: ctx.enter_context(nc.psum_tensor(f"{n}_add", shape, F32))
        sem = Sems(nc, ctx, "add")
        two_of = lambda n, shape, dt=F32: [sb(f"{n}{i}", shape, dt) for i in range(2)]
        gidx = two_of("gidx", [P, U], I32)
        srcs = two_of("srcs", [P, U, P], I32)
        wcol = two_of("wcol", [P, U])
        got_rows = two_of("got_rows", [P, U, W])
        mrow = two_of("mrow", [P, U, F])
        equal = two_of("equal", [P, U, P])
        dup = sb("dup", [P, U, P])
        cnt = sb("cnt", [P, 4, U])
        aidx = two_of("aidx", [P, U], I32)
        sumT = two_of("sumT", [P, U, KC, P])
        adds = two_of("adds", [P, U, W])
        ps_sum = pb("ps_sum", [P, U, KC, P])
        ps_add = pb("ps_add", [P, U, F])
        gidx_ready, srcs_in, got = sem("gidx_ready"), [sem(f"srcs_in{i}") for i in range(2)], [sem(f"got{i}") for i in range(2)]
        weighted, equal_ready, sums_done, sums_copied, adds_done, adds_ready, added = (
            sem("weighted"), sem("equal_ready"), sem("sums_done"), sem("sums_copied"), sem("adds_done"), sem("adds_ready"), sem("added"))
        released, marked, ch, wcol_ready = sem("released"), sem("marked"), sem("ch"), sem("wcol_ready")
        with nc.Block() as block:
            @block.gpsimd
            def _(pool):
                bound, dump_bound = pool.to_reg(EP - 1), pool.to_reg(NT - 1)

                def pick(r):
                    pool.wait_ge(gidx_ready, r.g + 1)
                    if r.reused:
                        pool.wait_ge(weighted, r.g - 1)
                    pool.sem_inc(released, 1)

                def gather(r, u):
                    nc.gpsimd.indirect_dma_start(
                        got_rows[r.b][:, u, :], None, m["gat1_rows"], bass.IndirectOffsetOnAxis(ap=gidx[r.b][:, u:u + 1], axis=0),
                        bounds_check=bound, oob_is_err=False).then_inc(got[r.b], 16)

                def add(r, u):
                    pool.wait_ge(adds_ready, r.g + 1)
                    pool.wait_ge(added, (r.g * U + u) * 16)
                    pool.sem_inc(released, 1)
                    nc.gpsimd.indirect_dma_start(
                        m["node_table"], bass.IndirectOffsetOnAxis(ap=aidx[r.b][:, u:u + 1], axis=0), adds[r.b][:, u, :], None,
                        bounds_check=dump_bound, oob_is_err=True, compute_op=ALU.add).then_inc(added, 16)

                def body(r):
                    pick(r)
                    for u in range(U):
                        gather(r, u)
                        if r.reused:
                            add(before(r), u)
                rounds(pool, body)
                for u in range(U):
                    add(LAST, u)
                pool.wait_ge(added, T * 16)

            @block.sync
            def _(sp):
                def load(r):
                    if r.reused:
                        sp.wait_ge(equal_ready, r.g - 1)
                    sp.dma_start(srcs[r.b][:, :, :].rearrange("p u q -> p (u q)"),
                                 m["src_rev_rows"][0:1, bass.ds(r.g * GE, GE)].partition_broadcast(P)).then_inc(srcs_in[r.b], 16)
                rounds(sp, load)

            @block.scalar
            def _(act):
                def body(r):
                    act.wait_ge(got[r.b], (r.n + 1) * U * 16)
                    act.wait_ge(wcol_ready, r.g + 1)
                    if r.reused:
                        act.wait_ge(sums_done, r.g - 1)
                    for u in range(U):
                        t = nc.scalar.activation(mrow[r.b][:, u, :], got_rows[r.b][:, u, 0:F], ACT.Copy,
                                                 scale=wcol[r.b][:, u:u + 1])
                    t.then_inc(weighted, 1)
                    act.wait_ge(sums_done, r.g + 1)
                    if r.reused:
                        act.wait_ge(adds_done, r.g - 1)
                    nc.scalar.activation(sumT[r.b][:, :, :, :], ps_sum[:, :, :, :], ACT.Copy).then_inc(sums_copied, 1)
                rounds(act, body)

            @block.vector
            def _(v):
                c = Vec(v, ch, 6)
                for b in range(2):
                    nc.vector.memset(adds[b][:, :, F:W], 0.0)
                nc.vector.memset(cnt[:, :, :], 0.0).then_inc(marked, 1)
                v.wait_ge(marked, 1)

                def prepare(r):
                    c.c.start(r.g)
                    if r.reused:
                        v.wait_ge(got[r.b], r.n * U * 16)
                    nc.vector.tensor_copy(gidx[r.b][:, :], m["run_end"][:, bass.ds(r.g * U, U)]).then_inc(gidx_ready, 1)
                    if r.reused:
                        v.wait_ge(weighted, r.g - 1)
                    nc.vector.tensor_copy(wcol[r.b][:, :], m["wrev"][:, bass.ds(r.g * U, U)]).then_inc(wcol_ready, 1)
                    v.wait_ge(srcs_in[r.b], (r.n + 1) * 16)
                    if r.reused:
                        v.wait_ge(sums_done, r.g - 1)
                    c.do(nc.vector.tensor_copy(cnt[:, 0, :], m["srcf_rev"][:, bass.ds(r.g * U, U)]))
                    c.wait()
                    nc.vector.tensor_tensor(equal[r.b][:, :, :], srcs[r.b][:, :, :],
                                            cnt[:, 0, :].unsqueeze(2).to_broadcast([P, U, P]), ALU.is_equal).then_inc(equal_ready, 1)
                    v.wait_ge(equal_ready, r.g + 1)
                    c.then(nc.vector.tensor_tensor(dup[:, :, :], equal[r.b][:, :, :],
                                                   m["later"][:, :].unsqueeze(1).to_broadcast([P, U, P]), ALU.mult))
                    c.do(nc.vector.tensor_reduce(cnt[:, 1, :], dup[:, :, :], AX.X, ALU.max))
                    c.then(nc.vector.tensor_scalar(cnt[:, 2, :], cnt[:, 0, :], -1.0, m["dump"][:, 0:1], ALU.mult, ALU.add))
                    c.then(nc.vector.tensor_tensor(cnt[:, 3, :], cnt[:, 2, :], cnt[:, 1, :], ALU.mult))
                    if r.reused:
                        v.wait_ge(added, (r.g - 1) * U * 16)
                    c.then(nc.vector.tensor_tensor(aidx[r.b][:, :], cnt[:, 3, :], cnt[:, 0, :], ALU.add))
                    c.c.end()

                def finish(r):
                    v.wait_ge(adds_done, r.g + 1)
                    if r.reused:
                        v.wait_ge(added, (r.g - 1) * U * 16)
                    nc.vector.tensor_copy(adds[r.b][:, :, 0:F], ps_add[:, :, :]).then_inc(adds_ready, 1)

                def body(r):
                    prepare(r)
                    finish(r)
                rounds(v, body)

            @block.tensor
            def _(pe):
                def body(r):
                    pe.wait_ge(weighted, r.g + 1)
                    pe.wait_ge(equal_ready, r.g + 1)
                    pe.wait_ge(sums_copied, r.g * 1)
                    for u in range(U):
                        for c in range(KC):
                            t = nc.tensor.matmul(ps_sum[:, u, c, :], mrow[r.b][:, u, c * P:(c + 1) * P], equal[r.b][:, u, :],
                                                 start=True, stop=True)
                    t.then_inc(sums_done, 1)
                    pe.wait_ge(sums_copied, r.g + 1)
                    pe.wait_ge(adds_ready, r.g * 1)
                    for u in range(U):
                        for c in range(KC):
                            t = nc.tensor.matmul(ps_add[:, u, :], sumT[r.b][:, u, c, :], w1t[:, c, :],
                                                 start=(c == 0), stop=(c == KC - 1))
                    t.then_inc(adds_done, 1)
                rounds(pe, body)
        sem.clear()


def last_phase(nc, m):
    ident, w3t = m["ident"], m["weights"]["w3t"]
    with ExitStack() as ctx:
        sb = lambda n, shape, dt=F32: ctx.enter_context(nc.sbuf_tensor(f"{n}_last", shape, dt))
        pb = lambda n, shape: ctx.enter_context(nc.psum_tensor(f"{n}_last", shape, F32))
        sem = Sems(nc, ctx, "last")
        two_of = lambda n, shape, dt=F32: [sb(f"{n}{i}", shape, dt) for i in range(2)]
        idx = two_of("idx", [P, 2 * U], I32)
        sidx = two_of("sidx", [P, U], I32)
        runs = two_of("runs", [P, 2, GE], I32)
        raw = two_of("raw", [P, U, W])
        own = two_of("own", [P, U, W])
        wcol = sb("wcol", [P, U])
        y2 = sb("y2", [P, U, F])
        part = sb("part", [P, U, F])
        mrow = sb("mrow", [P, U, F])
        same = sb("same", [P, GE])
        agg = sb("agg", [P, KC, GE])
        carry = sb("carry", [P, KC])
        z = sb("z", [P, U, F])
        orow = two_of("orow", [P, U, F])
        st = sb("st", [P, U, 6])
        wk, lnx = sb("wk", [P, 5, U]), sb("lnx", [P, 3, U])
        rs = [sb(f"rs{i}", [P, 2, U]) for i in range(3)]
        co = sb("co", [P, 4, U])
        turn = pb("turn", [P, KC, GE])
        ps_out = pb("ps_out", [P, U, F])
        idx_in, runs_in, got, own_in, written = ([sem(f"{n}{i}") for i in range(2)]
                                                 for n in ("idx_in", "runs_in", "got", "own_in", "written"))
        asked, half, rooted, co_ready, parts_ready, msgs_ready, turned, scans_done, prod_done, z_free = (
            sem(n) for n in ("asked", "half", "rooted", "co_ready", "parts_ready", "msgs_ready", "turned", "scans_done",
                             "prod_done", "z_free"))
        own_used, out_scaled, out_normed, sidx_ready, marked, ch, runs_read, released = (
            sem(n) for n in ("own_used", "out_scaled", "out_normed", "sidx_ready", "marked", "ch", "runs_read", "released"))
        with nc.Block() as block:
            @block.gpsimd
            def _(pool):
                bound = pool.to_reg(N - 1)

                def gather(r):
                    pool.wait_ge(idx_in[r.b], (r.n + 1) * 16)
                    if r.reused:
                        pool.wait_ge(msgs_ready, r.g - 1)
                    pool.sem_inc(released, 1)
                    for u in range(U):
                        nc.gpsimd.indirect_dma_start(
                            raw[r.b][:, u, :], None, m["node_table"][0:N, :],
                            bass.IndirectOffsetOnAxis(ap=idx[r.b][:, u:u + 1], axis=0),
                            bounds_check=bound, oob_is_err=False).then_inc(got[r.b], 16)

                def scatter(r):
                    pool.wait_ge(out_normed, r.g + 1)
                    pool.wait_ge(sidx_ready, r.g + 1)
                    pool.sem_inc(released, 1)
                    for u in range(U):
                        nc.gpsimd.indirect_dma_start(
                            m["out"], bass.IndirectOffsetOnAxis(ap=sidx[r.b][:, u:u + 1], axis=0), orow[r.b][:, u, :], None,
                            bounds_check=bound, oob_is_err=False).then_inc(written[r.b], 16)

                def body(r):
                    gather(r)
                    if r.reused:
                        scatter(before(r))
                rounds(pool, body)
                scatter(LAST)
                for b in range(2):
                    pool.wait_ge(written[b], (G + 1 - b) // 2 * U * 16)

            @block.sync
            def _(sp):
                def load(r):
                    if r.reused:
                        sp.wait_ge(runs_read, r.g - 1)
                        sp.wait_ge(own_used, r.g - 1)
                        sp.wait_ge(got[r.b], r.n * U * 16)
                    sp.dma_start(idx[r.b][:, :], m["pair_idx"][bass.ds(r.g, 1), :, :].rearrange("a p n -> (a p) n")
                                 ).then_inc(idx_in[r.b], 16)
                    for k in range(2):
                        sp.dma_start(runs[r.b][:, k, :], m["dst_run"][0:1, bass.ds(r.g * GE + k, GE)].partition_broadcast(P)
                                     ).then_inc(runs_in[r.b], 16)
                    sp.dma_start(own[r.b][:, :, :], m["gat2_rows"][bass.ds(r.g * GE, GE), :].rearrange("(u p) n -> p u n", p=P)
                                 ).then_inc(own_in[r.b], 16)
                rounds(sp, load)

            @block.scalar
            def _(act):
                def body(r):
                    for k in range(2):
                        root(nc, act, lnx, U, asked, r.g * 3 + k + 1, half, rooted)
                    act.wait_ge(co_ready, r.g + 1)
                    act.wait_ge(msgs_ready, r.g * 1)
                    for u in range(U):
                        t = nc.scalar.activation(part[:, u, :], raw[r.b][:, u, 0:F], ACT.Identity,
                                                 bias=co[:, 2, u:u + 1], scale=co[:, 0, u:u + 1])
                    t.then_inc(parts_ready, 1)
                    root(nc, act, lnx, U, asked, r.g * 3 + 3, half, rooted)
                    act.wait_ge(out_scaled, r.g + 1)
                    if r.reused:
                        act.wait_ge(written[r.b], r.n * U * 16)
                    for u in range(U):
                        t = nc.scalar.activation(orow[r.b][:, u, :], z[:, u, :], ACT.Identity,
                                                 bias=rs[2][:, 1, u:u + 1], scale=rs[2][:, 0, u:u + 1])
                    t.then_inc(out_normed, 1)
                rounds(act, body)

            @block.vector
            def _(v):
                c = Vec(v, ch, 4 * U + 3 * NORM_STEPS + 8)
                nc.vector.memset(carry[:, :], 0.0).then_inc(marked, 1)
                v.wait_ge(marked, 1)

                def body(r):
                    c.c.start(r.g)
                    if r.reused:
                        v.wait_ge(written[r.b], r.n * U * 16)
                    nc.vector.tensor_copy(sidx[r.b][:, :], m["last_idx"][:, bass.ds(r.g * U, U)]).then_inc(sidx_ready, 1)
                    c.do(nc.vector.tensor_copy(wcol[:, :], m["wcols"][:, bass.ds(r.g * U, U)]))
                    v.wait_ge(runs_in[r.b], (r.n + 1) * 32)
                    nc.vector.tensor_tensor(same[:, :], runs[r.b][:, 0, :], runs[r.b][:, 1, :], ALU.is_equal).then_inc(runs_read, 1)
                    v.wait_ge(got[r.b], (r.n + 1) * U * 16)
                    row = raw[r.b]
                    for u in range(U):
                        c.do(nc.vector.bn_stats(st[:, u, :], row[:, u, 0:F]))
                    c.wait()
                    norm_scalars(c, v, nc, st, wk, U, lnx, rs[0], asked, rooted, r.g * 3 + 1)
                    c.then(nc.vector.tensor_scalar(rs[0][:, 0, :], rs[0][:, 0, :], 2.0, None, ALU.mult))
                    for u in range(U):
                        c.do(nc.vector.scalar_tensor_tensor(out=y2[:, u, :], in0=row[:, u, 0:F], scalar=rs[0][:, 0, u:u + 1],
                                                            in1=m["elu_lnb"][:, :], op0=ALU.mult, op1=ALU.add))
                    c.wait()
                    for u in range(U):
                        c.do(nc.vector.bn_stats(st[:, u, :], y2[:, u, :]))
                    c.wait()
                    norm_scalars(c, v, nc, st, wk, U, lnx, rs[1], asked, rooted, r.g * 3 + 2)
                    c.then(minus_mean(nc, wk, rs[1], U))
                    mark = row[:, :, F]
                    c.then(nc.vector.tensor_tensor(co[:, 0, :], wcol[:, :], mark, ALU.mult))
                    c.then(nc.vector.tensor_tensor(co[:, 3, :], wcol[:, :], co[:, 0, :], ALU.subtract))
                    c.do(nc.vector.tensor_tensor(co[:, 1, :], co[:, 3, :], rs[1][:, 0, :], ALU.mult))
                    nc.vector.tensor_tensor(co[:, 2, :], co[:, 3, :], rs[1][:, 1, :], ALU.mult).then_inc(co_ready, 1)
                    v.wait_ge(co_ready, r.g + 1)
                    v.wait_ge(parts_ready, r.g + 1)
                    v.wait_ge(turned, r.g * 1)
                    for u in range(U):
                        t = nc.vector.scalar_tensor_tensor(out=mrow[:, u, :], in0=y2[:, u, :], scalar=co[:, 1, u:u + 1],
                                                           in1=part[:, u, :], op0=ALU.mult, op1=ALU.add)
                    t.then_inc(msgs_ready, 1)
                    v.wait_ge(msgs_ready, r.g + 1)
                    v.wait_ge(turned, r.g + 1)
                    v.wait_ge(prod_done, r.g * 1)
                    for k in range(KC):
                        t = nc.vector.tensor_tensor_scan(agg[:, k, :], same[:, :], turn[:, k, :], carry[:, k:k + 1], ALU.mult, ALU.add)
                    t.then_inc(scans_done, 1)
                    v.wait_ge(scans_done, r.g + 1)
                    c.do(nc.vector.tensor_copy(carry[:, :], agg[:, :, GE - 1]))
                    v.wait_ge(own_in[r.b], (r.n + 1) * 16)
                    v.wait_ge(prod_done, r.g + 1)
                    v.wait_ge(out_normed, r.g * 1)
                    nc.vector.tensor_tensor(z[:, :, :], ps_out[:, :, :], own[r.b][:, :, 0:F], ALU.add).then_inc(own_used, 1)
                    v.wait_ge(own_used, r.g + 1)
                    c.then(nc.vector.tensor_tensor(z[:, :, :], z[:, :, :], m["b3_b"][:, :].unsqueeze(1).to_broadcast([P, U, F]), ALU.add))
                    for u in range(U):
                        c.do(nc.vector.bn_stats(st[:, u, :], z[:, u, :]))
                    c.wait()
                    norm_scalars(c, v, nc, st, wk, U, lnx, rs[2], asked, rooted, r.g * 3 + 3)
                    minus_mean(nc, wk, rs[2], U).then_inc(out_scaled, 1)
                    v.wait_ge(out_scaled, r.g + 1)
                    c.c.end()
                rounds(v, body)

            @block.tensor
            def _(pe):
                def body(r):
                    pe.wait_ge(msgs_ready, r.g + 1)
                    pe.wait_ge(scans_done, r.g * 1)
                    for k in range(KC):
                        for u in range(U):
                            t = nc.tensor.transpose(turn[:, k, u * P:(u + 1) * P], mrow[:, u, k * P:(k + 1) * P], ident[:, :])
                    t.then_inc(turned, 1)
                    pe.wait_ge(scans_done, r.g + 1)
                    pe.wait_ge(own_used, r.g * 1)
                    for u in range(U):
                        for k in range(KC):
                            t = nc.tensor.matmul(ps_out[:, u, :], agg[:, k, u * P:(u + 1) * P], w3t[:, k, :],
                                                 start=(k == 0), stop=(k == KC - 1))
                    t.then_inc(prod_done, 1)
                rounds(pe, body)


def kernel(x, src, dst, edge_weight, L0_gnn_W_fc, L0_gnn_attn_l, L0_gnn_attn_r, L0_gnn_bias, L0_gnn_sem_W1,
           L0_gnn_sem_b1, L0_gnn_sem_W2, L1_gnn_W, L2_gnn_lin_w, L2_gnn_att, L2_gnn_ln_w, L2_gnn_ln_b, L3_gnn_W, L3_gnn_b):
    import concourse.bacc as bacc
    from concourse.bass_utils import run_bass_kernel_spmd

    c = lambda a: np.ascontiguousarray(np.asarray(a))

    def padded(a, fill):
        return np.concatenate([c(a), np.full(EP - E, fill, c(a).dtype)])

    s, d, w = padded(src, N), padded(dst, N), padded(edge_weight, 0)
    nxt = np.concatenate([d[1:], np.full(1, N + 1, d.dtype)])
    tiles = lambda a: c(a.reshape(T, P).T)
    back = lambda a: c(a[::-1].reshape(P, T))
    p = np.arange(P)
    arrays = {
        "x": c(x),
        "pair_idx": c(np.concatenate([s.reshape(G, U, P).transpose(0, 2, 1), d.reshape(G, U, P).transpose(0, 2, 1)], axis=2)),
        "dst_run": c(np.concatenate([np.full(1, -1, d.dtype), d])[None, :]),
        "dst_cols": tiles(d), "dst_next": tiles(nxt), "w_cols": tiles(w),
        "src_rev": back(s), "src_rev_rows": c(back(s).T.reshape(1, EP)), "dst_rev": back(d), "dst_next_rev": back(nxt),
        "w_rev": back(w), "pos_rev": back(np.arange(EP, dtype=np.float32)),
        "dump_col": (DUMP + p[:, None]).astype(np.float32),
        "ident_in": np.eye(P, dtype=np.float32),
        "heads_in": (np.arange(H)[:, None, None] == (np.arange(F) // D).reshape(1, KC, P)).astype(np.float32),
        "later_in": (p[None, :] > p[:, None]).astype(np.float32),
        "w_fc": c(L0_gnn_W_fc), "lin_w": c(L2_gnn_lin_w), "w1t": c(c(L1_gnn_W).T), "w3t": c(c(L3_gnn_W).T),
        "attn_l": c(L0_gnn_attn_l).reshape(1, F), "attn_r": c(L0_gnn_attn_r).reshape(1, F),
        "att": c(L2_gnn_att).reshape(1, 2 * F),
        "bias_row": c(L0_gnn_bias).reshape(1, F), "bias_cols": c(c(L0_gnn_bias).reshape(KC, P).T),
        "ln_w": c(L2_gnn_ln_w).reshape(1, F), "ln_b": c(L2_gnn_ln_b).reshape(1, F), "b3": c(L3_gnn_b).reshape(1, F),
    }
    nc = bacc.Bacc("TRN2", target_bir_lowering=False, num_devices=1)
    aps = {k: nc.dram_tensor(k + "_dram", a.shape, mybir.dt.from_np(a.dtype), kind="ExternalInput").ap()
           for k, a in arrays.items()}
    out = nc.dram_tensor("out_dram", (N, F), F32, kind="ExternalOutput").ap()
    build(nc, out=out, **aps)
    r = run_bass_kernel_spmd(nc, [{k + "_dram": a for k, a in arrays.items()}], core_ids=[0])
    return r.results[0]["out_dram"]
```

```python
from contextlib import ExitStack

import numpy as np

import concourse.bass as bass
from concourse import mybir

F32 = mybir.dt.float32
I32 = mybir.dt.int32
ALU = mybir.AluOpType
ACT = mybir.ActivationFunctionType
AX = mybir.AxisListType

N, E, F = 100000, 25000, 256
H, D = 8, 32
P = 128
KC = F // P
U = 4
GE = U * P
G = -(-E // GE)
EP = G * GE
T = EP // P
R = 16
NB = P * R
NF = N // NB
W = F + 1
DUMP = N + 8
NT = DUMP + GE
FAR = float(1 << 20)
NONE = 65536.0
LOW = -1.0e30
LN_EPS = 1e-5
SOFTMAX_EPS = 1e-16


class Sems:

    def __init__(self, nc, ctx, tag):
        self.nc, self.ctx, self.tag, self.all = nc, ctx, tag, []

    def __call__(self, name):
        self.all.append(self.ctx.enter_context(self.nc.semaphore(f"{name}_{self.tag}")))
        return self.all[-1]

    def clear(self):
        for sem in self.all:
            self.nc.gpsimd.sem_clear(sem)
        self.nc.all_engine_barrier()


class Steps:

    def __init__(self, eng, sem):
        self.eng, self.sem, self.total, self.entry, self.per = eng, sem, 0, None, 0

    def start(self, r):
        if not r.static and self.entry is None:
            self.entry = self.total
        if r.static and self.entry is not None:
            self.total, self.entry = self.entry + TURNS * 2 * self.per, None
        self.r, self.k = r, 0
        self.base = self.total if r.static else (r.g - HEAD) * self.per + self.entry

    def do(self, instruction):
        instruction.then_inc(self.sem, 1)
        self.k += 1

    def wait(self):
        self.eng.wait_ge(self.sem, self.base + self.k)

    def then(self, instruction):
        self.do(instruction)
        self.wait()

    def end(self):
        if self.r.static:
            self.total += self.k
            self.per = self.k if self.entry is None and self.r.g < HEAD else self.per
        assert self.r.static or self.k == self.per


HEAD = 3
TURNS = (G - 1 - HEAD - 2) // 2


class Round:

    def __init__(self, g, b, n):
        self.g, self.b, self.n = g, b, n
        self.static = isinstance(g, int)

    def at(self, k):
        return Round(self.g + k, (self.b + k) % 2, self.n + (self.b + k) // 2)

    def has(self, k):
        return not self.static or 0 <= self.g + k < G

    def past(self, k):
        return not self.static or self.g >= k


def rounds(eng, body, extra=0):
    for g in range(HEAD):
        body(Round(g, g % 2, g // 2))
    with eng.Fori(0, TURNS) as i:
        for k in range(2):
            g = HEAD + k
            body(Round(i * 2 + g, g % 2, i + g // 2))
    for g in range(HEAD + 2 * TURNS, G + extra):
        body(Round(g, g % 2, g // 2))


def block_rows(r):
    return N - NB if r.static and r.g == G - 1 else r.g * NB


def build(nc, x, pair_idx, dst_lin, dst_prev, dst_cols, dst_next, w_cols, src_rev, src_rev_rows, dst_rev, dst_next_rev,
          w_rev, pos_rev, dump_col, ident_in, heads_in, later_in, w_fc, lin_w, w1t, w3t, attn_l, attn_r, att,
          bias_row, bias_cols, ln_w, ln_b, b3, out):
    node_table = nc.dram_tensor("node_table", [NT, W], F32, kind="Internal").ap()
    gat1_rows = nc.dram_tensor("gat1_rows", [EP, W], F32, kind="Internal").ap()
    gat2_rows = nc.dram_tensor("gat2_rows", [EP, W], F32, kind="Internal").ap()
    run_same = nc.dram_tensor("run_same", [1, EP], F32, kind="Internal").ap()
    run_pen = nc.dram_tensor("run_pen", [1, EP], F32, kind="Internal").ap()

    whole = ExitStack()
    with whole:
        def keep(name, shape, dt=F32):
            return whole.enter_context(nc.sbuf_tensor(name, shape, dt))

        ident = keep("ident", [P, P])
        heads = keep("heads", [H, KC, P])
        weights = {}
        for name in ("fc", "lin", "w1t", "w3t"):
            weights[name] = keep(name, [P, KC, F])
        att_src = {name: keep("att_src_" + name, [P, KC, H]) for name in ("fc", "lin")}
        att_dst = {name: keep("att_dst_" + name, [P, KC, H]) for name in ("fc", "lin")}
        biasT = keep("biasT", [P, KC])
        elu_bias = keep("elu_bias", [P, F])
        elu_lnb = keep("elu_lnb", [P, F])
        lnw_b = keep("lnw_b", [P, F])
        lnb_b = keep("lnb_b", [P, F])
        b3_b = keep("b3_b", [P, F])
        last_idx = keep("last_idx", [P, T], I32)
        run_end = keep("run_end", [P, T], I32)
        srcf_rev = keep("srcf_rev", [P, T])
        wrev = keep("wrev", [P, T])
        wcols = keep("wcols", [P, T])
        later = keep("later", [P, U, GE])
        dump = keep("dump", [P, U])

        setup(nc, locals())
        gat_phase(nc, locals(), "fc", 1)
        scatter_phase(nc, locals(), gat1_rows, node_table, "gat1")
        add_phase(nc, locals())
        gat_phase(nc, locals(), "lin", 2)
        scatter_phase(nc, locals(), gat2_rows, node_table, "gat2")
        last_phase(nc, locals())


def setup(nc, m):
    with ExitStack() as ctx:
        sb = lambda name, shape, dt=F32: ctx.enter_context(nc.sbuf_tensor(name, shape, dt))
        sem = Sems(nc, ctx, "setup")
        att_rows = sb("att_rows", [P, 2, F])
        att_row2 = sb("att_row2", [P, H, 2 * D])
        bias_b = sb("bias_b", [P, F])
        prod = sb("prod", [P, KC, F])
        neg = sb("neg", [P, 2, F])
        ex = sb("ex", [P, 2, F])
        ints = sb("ints", [P, 7, T], I32)
        same = sb("same", [P, T])
        pen = sb("pen", [P, T])
        eq = sb("eq", [P, T])
        cand = sb("cand", [P, T])
        pos = sb("pos", [P, T])
        run_min = sb("run_min", [P, T])
        row = sb("row", [1, P + 1])
        row_min = sb("row_min", [1, P])
        one = sb("one", [1, 1])
        after = sb("after", [P, 1])
        zeros = sb("zeros", [(NT - N) // 5, 5 * W])
        ps_row = ctx.enter_context(nc.psum_tensor("ps_row", [1, P], F32))
        ps_col = ctx.enter_context(nc.psum_tensor("ps_col", [P, 1], F32))
        loaded, chain, neg_done, ex_done = sem("loaded"), sem("chain0"), sem("neg_done"), sem("ex_done")
        col_ready, row_done, row_ready, col_done, zeroed = (
            sem("col_ready"), sem("row_done"), sem("row_ready"), sem("col_done"), sem("zeroed"))
        dump_clear, pens_ready = sem("dump_clear"), sem("pens_ready")
        loads = [
            (m["ident"][:, :], m["ident_in"]), (m["heads"][:, :, :], m["heads_in"]), (m["later"][:, :, :], m["later_in"]),
            (m["dump"][:, :], m["dump_col"]), (m["biasT"][:, :], m["bias_cols"]),
            (m["wrev"][:, :], m["w_rev"]), (m["wcols"][:, :], m["w_cols"]), (pos[:, :], m["pos_rev"]),
            (ints[:, 0, :], m["dst_cols"]), (ints[:, 1, :], m["dst_next"]), (ints[:, 2, :], m["dst_rev"]),
            (ints[:, 3, :], m["dst_next_rev"]), (ints[:, 4, :], m["src_rev"]),
            (ints[:, 5, :], m["dst_lin"]), (ints[:, 6, :], m["dst_prev"]),
            (att_rows[:, 0, :], m["attn_l"].partition_broadcast(P)),
            (att_rows[:, 1, :], m["attn_r"].partition_broadcast(P)),
            (att_row2[:, :, :].rearrange("p h c -> p (h c)"), m["att"].partition_broadcast(P)),
            (bias_b[:, :], m["bias_row"].partition_broadcast(P)),
            (m["lnw_b"][:, :], m["ln_w"].partition_broadcast(P)),
            (m["lnb_b"][:, :], m["ln_b"].partition_broadcast(P)),
            (m["b3_b"][:, :], m["b3"].partition_broadcast(P)),
        ] + [(m["weights"][k][:, :, :], m[d].rearrange("(c p) n -> p c n", p=P))
             for k, d in (("fc", "w_fc"), ("lin", "lin_w"), ("w1t", "w1t"), ("w3t", "w3t"))]

        with nc.Block() as block:
            @block.sync
            def _(sp):
                for dst, src in loads:
                    sp.dma_start(dst, src).then_inc(loaded, 16)
                sp.wait_ge(zeroed, 1)
                sp.dma_start(m["node_table"][N:NT, :].rearrange("(p a) w -> p (a w)", a=5), zeros[:, :]).then_inc(dump_clear, 16)
                sp.wait_ge(pens_ready, 1)
                sp.dma_start(m["run_same"].rearrange("a (p t) -> (a p) t", p=P), same[:, :]).then_inc(dump_clear, 16)
                sp.dma_start(m["run_pen"].rearrange("a (p t) -> (a p) t", p=P), pen[:, :]).then_inc(dump_clear, 16)
                sp.wait_ge(dump_clear, 48)

            @block.scalar
            def _(act):
                nc.scalar.preload_act_table_set("natural_log_exp_and_others")
                act.wait_ge(loaded, 16 * len(loads))
                nc.scalar.activation(neg[:, 0, :], bias_b[:, :], ACT.Relu, scale=-1.0).then_inc(neg_done, 1)
                nc.scalar.activation(neg[:, 1, :], m["lnb_b"][:, :], ACT.Relu, scale=-1.0).then_inc(neg_done, 1)
                act.wait_ge(neg_done, 2)
                nc.scalar.activation(ex[:, :, :], neg[:, :, :], ACT.Exp, scale=-1.0).then_inc(ex_done, 1)

            @block.vector
            def _(v):
                c = Steps(v, chain)
                c.start(Round(0, 0, 0))
                nc.vector.memset(zeros[:, :], 0.0).then_inc(zeroed, 1)
                c.do(nc.vector.memset(row[0:1, 0:1], NONE))
                c.then(nc.vector.memset(one[:, :], 1.0))
                v.wait_ge(loaded, 16 * len(loads))
                c.then(nc.vector.tensor_tensor(eq[:, :], ints[:, 2, :], ints[:, 3, :], ALU.is_equal))
                c.then(nc.vector.scalar_tensor_tensor(out=cand[:, :], in0=eq[:, :], scalar=NONE, in1=pos[:, :],
                                                      op0=ALU.mult, op1=ALU.add))
                nc.vector.tensor_tensor_scan(run_min[:, :], cand[:, :], cand[:, :], NONE, ALU.min,
                                             ALU.min).then_inc(col_ready, 1)
                c.then(nc.vector.tensor_tensor(same[:, :], ints[:, 5, :], ints[:, 6, :], ALU.is_equal))
                nc.vector.tensor_scalar(pen[:, :], same[:, :], -LOW, LOW, ALU.mult, ALU.add).then_inc(pens_ready, 1)
                for name, parts in (("fc", (att_rows[:, 0, :], att_rows[:, 1, :])),
                                    ("lin", (att_row2[:, :, D:2 * D], att_row2[:, :, 0:D]))):
                    for goal, part in zip((m["att_src"][name], m["att_dst"][name]), parts):
                        for k in range(KC):
                            a, w = prod[:, k, :], m["weights"][name][:, k, :]
                            if name == "lin":
                                a, w = (t.rearrange("p (h c) -> p h c", h=H) for t in (a, w))
                            c.then(nc.vector.tensor_tensor(a, w, part, ALU.mult))
                            c.then(nc.vector.tensor_reduce(goal[:, k, :], prod[:, k, :].rearrange("p (h c) -> p h c", h=H),
                                                           AX.X, ALU.add))
                v.wait_ge(ex_done, 1)
                for k, (goal, b) in enumerate(((m["elu_bias"], bias_b), (m["elu_lnb"], m["lnb_b"]))):
                    c.do(nc.vector.scalar_tensor_tensor(out=goal[:, :], in0=ex[:, k, :], scalar=-1.0, in1=b[:, :],
                                                        op0=ALU.add, op1=ALU.max))
                c.then(nc.vector.tensor_tensor(eq[:, :], ints[:, 0, :], ints[:, 1, :], ALU.is_equal))
                c.then(nc.vector.scalar_tensor_tensor(out=cand[:, :], in0=eq[:, :], scalar=FAR, in1=ints[:, 0, :],
                                                      op0=ALU.mult, op1=ALU.add))
                c.do(nc.vector.tensor_copy(m["last_idx"][:, :], cand[:, :]))
                c.do(nc.vector.tensor_copy(m["srcf_rev"][:, :], ints[:, 4, :]))
                v.wait_ge(row_done, 1)
                c.then(nc.vector.tensor_copy(row[0:1, 1:P + 1], ps_row[0:1, :]))
                nc.vector.tensor_tensor_scan(row_min[0:1, :], row[0:1, 0:P], row[0:1, 0:P], NONE, ALU.min,
                                             ALU.min).then_inc(row_ready, 1)
                v.wait_ge(col_done, 1)
                c.then(nc.vector.tensor_copy(after[:, :], ps_col[:, :]))
                c.then(nc.vector.tensor_scalar(cand[:, :], run_min[:, :], after[:, 0:1], None, ALU.min))
                c.then(nc.vector.tensor_copy(m["run_end"][:, :], cand[:, :]))

            @block.tensor
            def _(pe):
                pe.wait_ge(loaded, 16 * len(loads))
                pe.wait_ge(col_ready, 1)
                nc.tensor.matmul(ps_row[0:1, :], run_min[:, T - 1:T], m["ident"][:, :], start=True,
                                 stop=True).then_inc(row_done, 1)
                pe.wait_ge(row_ready, 1)
                nc.tensor.matmul(ps_col[:, 0:1], row_min[0:1, :], one[0:1, 0:1], start=True, stop=True).then_inc(col_done, 1)
        sem.clear()


def norm_chain(nc, c, st, wk, half, n, rs, done):
    g = nc.gpsimd
    me, cve, mo, cvo = st[:, 0:n, 1], st[:, 0:n, 2], st[:, 0:n, 4], st[:, 0:n, 5]
    d, cv, s = wk[:, 0, 0:n], wk[:, 1, 0:n], wk[:, 2, 0:n]
    c.do(g.tensor_tensor(d, me, mo, ALU.subtract))
    c.do(g.tensor_tensor(cv, cve, cvo, ALU.add))
    c.then(g.tensor_tensor(s, me, mo, ALU.add))
    c.do(g.tensor_tensor(wk[:, 3, 0:n], d, half[:, 0:n], ALU.mult))
    c.do(g.tensor_scalar(wk[:, 4, 0:n], cv, 1.0 / F, LN_EPS, ALU.mult, ALU.add))
    c.then(g.tensor_scalar(wk[:, 5, 0:n], s, -0.5, None, ALU.mult))
    c.then(g.tensor_tensor(wk[:, 3, 0:n], wk[:, 3, 0:n], wk[:, 3, 0:n], ALU.mult))
    c.then(g.tensor_tensor(wk[:, 4, 0:n], wk[:, 4, 0:n], wk[:, 3, 0:n], ALU.add))
    c.then(g.tensor_tensor(rs[:, 0, 0:n], wk[:, 4, 0:n], half[:, 0:n], ALU.pow))
    g.tensor_tensor(rs[:, 1, 0:n], wk[:, 5, 0:n], rs[:, 0, 0:n], ALU.mult).then_inc(done, 1)


def gat_phase(nc, m, name, layer):
    two = layer == 2
    RW = W if two else F
    ends = m["node_table"][0:N, :] if two else m["x"]
    kept = m["gat2_rows"] if two else m["gat1_rows"]
    ident, heads, wgt = m["ident"], m["heads"], m["weights"][name]
    a_src, a_dst = m["att_src"][name], m["att_dst"][name]
    with ExitStack() as ctx:
        sb = lambda n, shape, dt=F32: ctx.enter_context(nc.sbuf_tensor(f"{n}_{layer}", shape, dt))
        pb = lambda n, shape: ctx.enter_context(nc.psum_tensor(f"{n}_{layer}", shape, F32))
        sem = Sems(nc, ctx, layer)
        two_of = lambda n, shape, dt=F32: [sb(f"{n}{i}", shape, dt) for i in range(2)]
        two_sems = lambda n: [sem(f"{n}{i}") for i in range(2)]

        idx = two_of("idx", [P, 2 * U], I32)
        pen = two_of("pen", [H, GE])
        raw = two_of("raw", [P, 2 * U, RW])
        rows = two_of("rows", [P, 2 * U, F]) if two else raw
        srcT = sb("srcT", [P, KC, GE])
        dstT = [sb("dstT", [P, KC, GE])] * 2 if two else two_of("dstT", [P, KC, GE])
        logit = sb("logit", [P, U * H])
        leaky = sb("leaky", [P, U * H])
        top = sb("top", [H, GE + 1])
        before_top = sb("before_top", [H, GE])
        diff = sb("diff", [H, 2, GE])
        probs = sb("probs", [H, 2, GE])
        den = sb("den", [H, GE + 1])
        rdenT = sb("rdenT", [P, U, H])
        wide = sb("wide", [P, U, F])
        pcopy = sb("pcopy", [P, KC, GE])
        msg = sb("msg", [P, KC, GE])
        agg = sb("agg", [P, KC, GE])
        carry = sb("carry", [P, KC])
        yT = sb("yT", [P, KC, GE])
        if two:
            yrow = sb("yrow", [P, U, F])
            y2row = sb("y2row", [P, U, F])
            erow = sb("erow", [P, U, F])
        else:
            yb = sb("yb", [P, KC, GE])
            eT = sb("eT", [P, KC, GE])
        kept_rows = two_of("kept_rows", [P, U, W])
        st_f, st_t, st_u = sb("st_f", [P, 2 * U, 6]), sb("st_t", [P, U, 6]), sb("st_u", [P, U, 6])
        rs_f, rs_t, rs_u = sb("rs_f", [P, 2, 2 * U]), sb("rs_t", [P, 2, U]), sb("rs_u", [P, 2, U])
        wk, half = sb("wk", [P, 6, R]), sb("half", [P, R])
        xb = two_of("xb", [P, R, RW])
        ob = two_of("ob", [P, R, W if not two else F])
        st_d = [sb(f"st_d{k}", [P, R, 6]) for k in range(3 if two else 1)]
        rs_d = [sb(f"rs_d{k}", [P, 2, R]) for k in range(3 if two else 1)]

        turn = pb("turn", [P, KC, GE])
        ps_heads = turn[0:H, 0, :]
        ps_logit = turn[:, 1, 0:U * H]
        ps_den = turn[:, 1, 2 * U * H:3 * U * H]
        feat = pb("feat", [P, KC, GE])
        bcast = [pb(f"bcast{c}", [P, GE]) for c in range(KC)]
        back = pb("back", [P, U, F])

        idx_in, pen_in, got, kept_out, x_in, o_out = (
            two_sems(n) for n in ("idx_in", "pen_in", "got", "kept_out", "x_in", "o_out"))
        marked, released = sem("marked"), sem("released")
        turned, copied, logits_done, logits_turned, leaky_ready, feats_done = (
            sem(n) for n in ("turned", "copied", "logits_done", "logits_turned", "leaky_ready", "feats_done"))
        wide_ready, pen_read, diffs_ready, exps_ready, dens_ready, dens_turned, rden_ready = (
            sem(n) for n in ("wide_ready", "pen_read", "diffs_ready", "exps_ready", "dens_ready", "dens_turned", "rden_ready"))
        spread, p_copied, msgs_done, scans_done, scaled, biased, negs, exps, y_ready, turned_back = (
            sem(n) for n in ("spread", "p_copied", "msgs_done", "scans_done", "scaled", "biased", "negs", "exps",
                             "y_ready", "turned_back"))
        t_stats, t_scalars, t_normed = sem("t_stats"), sem("t_scalars"), sem("t_normed")
        f_stats, f_scalars, rows_normed = sem("f_stats"), sem("f_scalars"), sem("rows_normed")
        affine, o_neg, o_exp, y2_done, u_stats, u_scalars, u_normed = (
            sem(n) for n in ("affine", "o_neg", "o_exp", "y2_done", "u_stats", "u_scalars", "u_normed"))
        x_lifted, x_added, v_added, x_scaled, d_normed = (
            sem(n) for n in ("x_lifted", "x_added", "v_added", "x_scaled", "d_normed"))
        d_stats = [sem(f"d_stats{k}") for k in range(3 if two else 1)]
        d_scalars = [sem(f"d_scalars{k}") for k in range(3 if two else 1)]
        vec_m, vec_t, vec_d, pool_n = sem("vec_m"), sem("vec_t"), sem("vec_d"), sem("pool_n")
        done = u_normed if two else t_normed
        row_of = lambda t, n: t[:, :].unsqueeze(1).to_broadcast([P, n, F])

        with nc.Block() as block:
            @block.gpsimd
            def _(pool):
                bound = pool.to_reg(N - 1)
                c = Steps(pool, pool_n)
                nc.gpsimd.memset(half[:, :], -0.5).then_inc(released, 1)
                pool.wait_ge(released, 1)

                def gathers(r, js):
                    if js[0] == 0:
                        pool.wait_ge(idx_in[r.b], (r.n + 1) * 16)
                        if r.past(2):
                            pool.wait_ge(rows_normed if two else turned, (r.g - 1) * 2)
                    pool.sem_inc(released, 1)
                    for j in js:
                        nc.gpsimd.indirect_dma_start(
                            raw[r.b][:, j, :], None, ends, bass.IndirectOffsetOnAxis(ap=idx[r.b][:, j:j + 1], axis=0),
                            bounds_check=bound, oob_is_err=False).then_inc(got[r.b], 16)

                def norm(r, st, n, rs, stats, used, scalars, uses=1):
                    pool.wait_ge(stats, r.g + 1)
                    if r.past(1):
                        pool.wait_ge(used, r.g * uses)
                    norm_chain(nc, c, st, wk, half, n, rs, scalars)
                    pool.wait_ge(scalars, r.g + 1)

                def add_row(r, plus, ready, value):
                    n = R if two else R // 2
                    pool.wait_ge(ready, value)
                    if r.past(2):
                        pool.wait_ge(o_out[r.b], r.n * 16)
                    nc.gpsimd.tensor_tensor(ob[r.b][:, 0:n, 0:F], xb[r.b][:, 0:n, 0:F], row_of(plus, n), ALU.add).then_inc(x_added, 1)

                def body(r):
                    c.start(r)
                    if two:
                        if r.has(2):
                            gathers(r.at(2), range(U, 2 * U))
                        if r.has(0):
                            norm(r, st_d[0], R, rs_d[0], d_stats[0], x_lifted, d_scalars[0])
                        if r.has(-2):
                            norm(r.at(-2), st_d[2], R, rs_d[2], d_stats[2], d_normed, d_scalars[2])
                        if r.has(-1):
                            norm(r.at(-1), st_u, U, rs_u, u_stats, u_normed, u_scalars)
                            add_row(r.at(-1), m["b3_b"], x_scaled, r.g)
                        if r.has(3):
                            gathers(r.at(3), range(U))
                        if r.has(0):
                            norm(r, st_d[1], R, rs_d[1], d_stats[1], x_scaled, d_scalars[1])
                            norm(r, st_t, U, rs_t, t_stats, t_normed, t_scalars)
                        if r.has(2):
                            norm(r.at(2), st_f, 2 * U, rs_f, f_stats, rows_normed, f_scalars, 2)
                    else:
                        if r.has(2):
                            gathers(r.at(2), range(2 * U))
                        if r.has(-1):
                            norm(r.at(-1), st_d[0], R, rs_d[0], d_stats[0], d_normed, d_scalars[0])
                            norm(r.at(-1), st_t, U, rs_t, t_stats, t_normed, t_scalars)
                        if r.has(0):
                            add_row(r, m["elu_bias"], x_in[r.b], (r.n + 1) * 16)
                    c.end()

                first = Round(0, 0, 0)
                for r in (first, first.at(1)):
                    gathers(r, range(2 * U))
                if two:
                    for r in (first, first.at(1)):
                        c.start(Round(0, 0, 0))
                        norm(r, st_f, 2 * U, rs_f, f_stats, rows_normed, f_scalars, 2)
                        c.end()
                    gathers(first.at(2), range(U))
                rounds(pool, body, 2 if two else 1)

            @block.sync
            def _(sp):
                def load_edges(r):
                    if r.past(2):
                        sp.wait_ge(got[r.b], r.n * 2 * U * 16)
                    sp.dma_start(idx[r.b][:, :], m["pair_idx"][bass.ds(r.g, 1), :, :].rearrange("a p n -> (a p) n")
                                 ).then_inc(idx_in[r.b], 16)

                def load_pen(r):
                    if r.past(2):
                        sp.wait_ge(pen_read, r.g - 1)
                    sp.dma_start(pen[r.b][:, :], m["run_pen"][0:1, bass.ds(r.g * GE, GE)].partition_broadcast(H)
                                 ).then_inc(pen_in[r.b], 16)

                def load_nodes(r):
                    if r.past(2):
                        sp.wait_ge(x_added, r.g - 1)
                        if not two:
                            sp.wait_ge(v_added, r.g - 1)
                    src = m["node_table"] if two else m["x"]
                    sp.dma_start(xb[r.b][:, :, :], src[bass.ds(block_rows(r), NB), :].rearrange("(p r) n -> p r n", p=P)
                                 ).then_inc(x_in[r.b], 16)

                def store(r):
                    dst = m["out"] if two else m["node_table"]
                    sp.wait_ge(d_normed, r.g + 1)
                    if r.static and r.g == G - 1:
                        sp.wait_ge(o_out[1 - r.b], (r.n + r.b) * 16)
                    sp.dma_start(dst[bass.ds(block_rows(r), NB), :].rearrange("(p r) n -> p r n", p=P), ob[r.b][:, :, :]
                                 ).then_inc(o_out[r.b], 16)

                def store_rows(r):
                    sp.wait_ge(done, r.g + 1)
                    sp.dma_start(kept[bass.ds(r.g * GE, GE), :].rearrange("(u p) n -> p u n", p=P), kept_rows[r.b][:, :, :]
                                 ).then_inc(kept_out[r.b], 16)

                def body(r):
                    if r.has(3):
                        load_edges(r.at(3))
                    if r.has(2):
                        load_pen(r.at(2))
                    if not two and r.has(1):
                        load_nodes(r.at(1))
                    if r.has(-1):
                        store_rows(r.at(-1))
                    if two and r.has(1):
                        load_nodes(r.at(1))
                    if r.has(-2 if two else -1):
                        store(r.at(-2 if two else -1))

                first = Round(0, 0, 0)
                load_edges(first)
                load_edges(first.at(1))
                load_pen(first)
                load_pen(first.at(1))
                load_nodes(first)
                load_edges(first.at(2))
                sp.wait_ge(marked, 1)
                rounds(sp, body, 2 if two else 1)
                for b in range(2):
                    sp.wait_ge(kept_out[b], (G + 1 - b) // 2 * 16)
                    sp.wait_ge(o_out[b], (G + 1 - b) // 2 * 16)

            @block.tensor
            def _(pe):
                def turn_side(r, side):
                    if side == 0:
                        if two:
                            pe.wait_ge(rows_normed, r.g * 2 + 1)
                        else:
                            pe.wait_ge(got[r.b], (r.n + 1) * 2 * U * 16)
                        if r.past(1):
                            pe.wait_ge(diffs_ready, r.g)
                            pe.wait_ge(rden_ready, r.g)
                    else:
                        if two:
                            pe.wait_ge(rows_normed, r.g * 2 + 2)
                        pe.wait_ge(copied, r.g * 2 + 1)
                    for c in range(KC):
                        for u in range(U):
                            t = nc.tensor.transpose(turn[:, c, u * P:(u + 1) * P],
                                                    rows[r.b][:, side * U + u, c * P:(c + 1) * P], ident[:, :])
                    t.then_inc(turned, 1)

                def logits(r):
                    pe.wait_ge(copied, r.g * 2 + 2)
                    for u in range(U):
                        for k in range(2 * KC):
                            s = k < KC
                            t = nc.tensor.matmul(ps_logit[:, u * H:(u + 1) * H],
                                                 (srcT if s else dstT[r.b])[:, k % KC, u * P:(u + 1) * P],
                                                 (a_src if s else a_dst)[:, k % KC, :], start=(k == 0), stop=(k == 2 * KC - 1))
                    t.then_inc(logits_done, 1)

                def turn_logits(r):
                    pe.wait_ge(leaky_ready, r.g + 1)
                    for u in range(U):
                        t = nc.tensor.matmul(ps_heads[:, u * P:(u + 1) * P], leaky[:, u * H:(u + 1) * H], ident[:, :],
                                             start=True, stop=True)
                    t.then_inc(logits_turned, 1)

                def features(r):
                    if r.past(1):
                        pe.wait_ge(msgs_done, r.g * 2)
                    for c in range(KC):
                        for k in range(KC):
                            t = nc.tensor.matmul(feat[:, c, :], wgt[:, k, c * P:(c + 1) * P], srcT[:, k, :],
                                                 start=(k == 0), stop=(k == KC - 1))
                    t.then_inc(feats_done, 1)

                def spread_probs(r):
                    pe.wait_ge(exps_ready, r.g + 1)
                    for c in range(KC):
                        if r.past(1):
                            pe.wait_ge(scaled, r.g * 2 - 1 + c)
                        nc.tensor.matmul(bcast[c][:, :], heads[:, c, :], probs[:, 1, :], start=True, stop=True).then_inc(spread, 1)

                def spread_decays(r):
                    for c in range(KC):
                        pe.wait_ge(p_copied, r.g * 2 + c + 1)
                        nc.tensor.matmul(bcast[c][:, :], heads[:, c, :], probs[:, 0, :], start=True, stop=True).then_inc(spread, 1)

                def turn_sums(r):
                    pe.wait_ge(dens_ready, r.g + 1)
                    for u in range(U):
                        t = nc.tensor.matmul(ps_den[:, u * H:(u + 1) * H], den[:, 1 + u * P:1 + (u + 1) * P], ident[0:H, 0:H],
                                             start=True, stop=True)
                    t.then_inc(dens_turned, 1)

                def spread_rden(r):
                    pe.wait_ge(wide_ready, r.g + 1)
                    for c in range(KC):
                        pe.wait_ge(scans_done, r.g * 2 + c + 1)
                        for u in range(U):
                            t = nc.tensor.matmul(bcast[c][:, u * P:(u + 1) * P], wide[:, u, c * P:(c + 1) * P], ident[:, :],
                                                 start=True, stop=True)
                        t.then_inc(spread, 1)

                def turn_back(r):
                    if two:
                        pe.wait_ge(scaled, r.g * 2 + 2)
                    else:
                        pe.wait_ge(y_ready, r.g + 1)
                    if r.past(1):
                        pe.wait_ge(t_normed, r.g)
                    for u in range(U):
                        for c in range(KC):
                            t = nc.tensor.transpose(back[:, u, c * P:(c + 1) * P], yT[:, c, u * P:(u + 1) * P], ident[:, :])
                    t.then_inc(turned_back, 1)

                def body(r):
                    if r.has(0):
                        spread_probs(r)
                    if not two and r.has(-1):
                        turn_back(r.at(-1))
                    if two:
                        spread_decays(r)
                        spread_rden(r)
                        turn_back(r)
                        if r.has(1):
                            turn_side(r.at(1), 0)
                            turn_side(r.at(1), 1)
                            logits(r.at(1))
                            turn_logits(r.at(1))
                            features(r.at(1))
                            turn_sums(r.at(1))
                    else:
                        if r.has(1):
                            turn_side(r.at(1), 0)
                        if r.has(0):
                            spread_decays(r)
                        if r.has(1):
                            turn_side(r.at(1), 1)
                        if r.has(0):
                            spread_rden(r)
                        if r.has(1):
                            logits(r.at(1))
                            turn_logits(r.at(1))
                            features(r.at(1))
                            turn_sums(r.at(1))

                first = Round(0, 0, 0)
                turn_side(first, 0)
                turn_side(first, 1)
                logits(first)
                turn_logits(first)
                features(first)
                turn_sums(first)
                rounds(pe, body, 0 if two else 1)

            @block.scalar
            def _(act):
                nc.scalar.preload_act_table_set("natural_log_exp_and_others")

                def norm_rows(r):
                    act.wait_ge(f_scalars, r.g + 1)
                    if r.past(1):
                        act.wait_ge(turned, r.g * 2)
                    if r.past(2):
                        act.wait_ge(y2_done, r.g - 1)
                    for j in range(2 * U):
                        t = nc.scalar.activation(rows[r.b][:, j, :], raw[r.b][:, j, 0:F], ACT.Identity,
                                                 bias=rs_f[:, 1, j:j + 1], scale=rs_f[:, 0, j:j + 1])
                        if j % U == U - 1:
                            t.then_inc(rows_normed, 1)

                def copy_side(r, side):
                    act.wait_ge(turned, r.g * 2 + 1 + side)
                    if side == 0 and r.past(1):
                        act.wait_ge(feats_done, r.g)
                    if side == 1 and r.past(2) and not two:
                        act.wait_ge(y_ready, r.g - 1)
                    nc.scalar.activation((dstT[r.b] if side else srcT)[:, :, :], turn[:, :, :], ACT.Copy).then_inc(copied, 1)

                def probabilities(r):
                    act.wait_ge(diffs_ready, r.g + 1)
                    if r.past(1):
                        act.wait_ge(spread, r.g * 6 - 2)
                        act.wait_ge(dens_ready, r.g)
                    nc.scalar.activation(probs[:, :, :], diff[:, :, :], ACT.Exp).then_inc(exps_ready, 1)

                def copy_probs(r):
                    for c in range(KC):
                        act.wait_ge(spread, r.g * 6 + c + 1)
                        if r.past(1):
                            act.wait_ge(msgs_done, r.g * 2)
                        nc.scalar.activation(pcopy[:, c, :], bcast[c][:, :], ACT.Copy).then_inc(p_copied, 1)

                def widen(r):
                    act.wait_ge(rden_ready, r.g + 1)
                    if r.past(1):
                        act.wait_ge(spread, r.g * 6)
                    nc.scalar.activation(wide[:, :, :].rearrange("p u (h c) -> p (u h) c", c=D),
                                         rdenT[:, :, :].rearrange("p u h -> p (u h)").unsqueeze(2).to_broadcast([P, U * H, D]),
                                         ACT.Copy).then_inc(wide_ready, 1)

                def elu_parts(r):
                    for c in range(KC):
                        act.wait_ge(scaled, r.g * 2 + c + 1)
                        if r.past(1):
                            act.wait_ge(y_ready, r.g)
                        nc.scalar.activation(yb[:, c, :], agg[:, c, :], ACT.Identity,
                                             bias=m["biasT"][:, c:c + 1]).then_inc(biased, 1)
                    act.wait_ge(biased, r.g * 2 + 2)
                    nc.scalar.activation(eT[:, :, :], yb[:, :, :], ACT.Relu, scale=-1.0).then_inc(negs, 1)
                    act.wait_ge(negs, r.g + 1)
                    nc.scalar.activation(eT[:, :, :], eT[:, :, :], ACT.Exp, scale=-1.0).then_inc(exps, 1)

                def norm_back(r):
                    act.wait_ge(t_scalars, r.g + 1)
                    if r.past(2) and not two:
                        act.wait_ge(kept_out[r.b], r.n * 16)
                    if two and r.past(1):
                        act.wait_ge(y2_done, r.g)
                    goal = yrow if two else kept_rows[r.b]
                    for u in range(U):
                        t = nc.scalar.activation(goal[:, u, 0:F], back[:, u, :], ACT.Identity,
                                                 bias=rs_t[:, 1, u:u + 1], scale=rs_t[:, 0, u:u + 1])
                    t.then_inc(t_normed, 1)

                def elu_rows(r):
                    act.wait_ge(affine, r.g + 1)
                    nc.scalar.activation(erow[:, :, :], yrow[:, :, :], ACT.Relu, scale=-1.0).then_inc(o_neg, 1)
                    act.wait_ge(o_neg, r.g + 1)
                    nc.scalar.activation(erow[:, :, :], erow[:, :, :], ACT.Exp, scale=-1.0).then_inc(o_exp, 1)

                def norm_kept(r):
                    act.wait_ge(u_scalars, r.g + 1)
                    if r.past(2):
                        act.wait_ge(kept_out[r.b], r.n * 16)
                    for u in range(U):
                        t = nc.scalar.activation(kept_rows[r.b][:, u, 0:F], y2row[:, u, :], ACT.Identity,
                                                 bias=rs_u[:, 1, u:u + 1], scale=rs_u[:, 0, u:u + 1])
                    t.then_inc(u_normed, 1)

                def scale_nodes(r, js):
                    act.wait_ge(d_scalars[1], r.g + 1)
                    for j in js:
                        t = nc.scalar.activation(xb[r.b][:, j, 0:F], xb[r.b][:, j, 0:F], ACT.Copy,
                                                 scale=rs_d[1][:, 0, j:j + 1])
                    if js[-1] == R - 1:
                        t.then_inc(x_scaled, 1)

                def norm_nodes(r, js):
                    act.wait_ge(d_scalars[2 if two else 0], r.g + 1)
                    rs = rs_d[2 if two else 0]
                    for j in js:
                        t = nc.scalar.activation(ob[r.b][:, j, 0:F], ob[r.b][:, j, 0:F], ACT.Identity,
                                                 bias=rs[:, 1, j:j + 1], scale=rs[:, 0, j:j + 1])
                    if js[-1] == R - 1:
                        t.then_inc(d_normed, 1)

                part = range(R // 2), range(R // 2, R)

                def body(r):
                    if two and r.has(-1):
                        norm_back(r.at(-1))
                    if r.has(0):
                        copy_probs(r)
                    if two:
                        if r.has(0):
                            widen(r)
                        if r.has(-1):
                            scale_nodes(r.at(-1), part[0])
                            elu_rows(r.at(-1))
                            scale_nodes(r.at(-1), part[1])
                        if r.has(1):
                            norm_rows(r.at(1))
                        if r.has(-1):
                            norm_kept(r.at(-1))
                        if r.has(1):
                            copy_side(r.at(1), 0)
                            copy_side(r.at(1), 1)
                        if r.has(-2):
                            norm_nodes(r.at(-2), part[0])
                            norm_nodes(r.at(-2), part[1])
                        if r.has(1):
                            probabilities(r.at(1))
                    else:
                        if r.has(1):
                            copy_side(r.at(1), 0)
                        if r.has(0):
                            widen(r)
                        if r.has(1):
                            copy_side(r.at(1), 1)
                        if r.has(-1):
                            norm_nodes(r.at(-1), part[0])
                        if r.has(0):
                            elu_parts(r)
                        if r.has(1):
                            probabilities(r.at(1))
                        if r.has(-1):
                            norm_back(r.at(-1))
                            norm_nodes(r.at(-1), part[1])

                first = Round(0, 0, 0)
                if two:
                    norm_rows(first)
                copy_side(first, 0)
                copy_side(first, 1)
                probabilities(first)
                rounds(act, body, 2 if two else 1)

            @block.vector
            def _(v):
                cm, ct, cd = Steps(v, vec_m), Steps(v, vec_t), Steps(v, vec_d)
                if not two:
                    for b in range(2):
                        nc.vector.memset(ob[b][:, :, F:W], 0.0)
                for b in range(2):
                    nc.vector.memset(kept_rows[b][:, :, F:W], 1.0 if two else 0.0)
                nc.vector.memset(carry[:, :], 0.0)
                nc.vector.memset(den[:, GE:GE + 1], 0.0)
                nc.vector.memset(top[:, GE:GE + 1], 0.0).then_inc(marked, 1)
                v.wait_ge(marked, 1)

                def stats(r, st, src, n, ready, read, first=0, last=True):
                    if r.past(1):
                        v.wait_ge(read, r.g)
                    for j in range(first, n):
                        t = nc.vector.bn_stats(st[:, j, :], src[:, j, 0:F])
                    if last:
                        t.then_inc(ready, 1)

                def leaks(r):
                    v.wait_ge(logits_done, r.g + 1)
                    cm.then(nc.vector.tensor_copy(logit[:, :], ps_logit))
                    if r.past(1):
                        v.wait_ge(logits_turned, r.g)
                    nc.vector.scalar_tensor_tensor(out=leaky[:, :], in0=logit[:, :], scalar=0.2, in1=logit[:, :],
                                                   op0=ALU.mult, op1=ALU.max).then_inc(leaky_ready, 1)

                def maxima(r):
                    cm.then(nc.vector.tensor_copy(top[:, 0:1], top[:, GE:GE + 1]))
                    v.wait_ge(pen_in[r.b], (r.n + 1) * 16)
                    v.wait_ge(logits_turned, r.g + 1)
                    cm.then(nc.vector.tensor_tensor_scan(top[:, 1:GE + 1], pen[r.b][:, :], ps_heads, top[:, 0:1],
                                                         ALU.add, ALU.max))
                    if r.past(1):
                        v.wait_ge(exps_ready, r.g)
                    cm.do(nc.vector.tensor_tensor(diff[:, 1, :], ps_heads, top[:, 1:GE + 1], ALU.subtract))
                    nc.vector.tensor_tensor(before_top[:, :], pen[r.b][:, :], top[:, 0:GE], ALU.add).then_inc(pen_read, 1)
                    v.wait_ge(pen_read, r.g + 1)
                    nc.vector.tensor_tensor(diff[:, 0, :], before_top[:, :], top[:, 1:GE + 1], ALU.subtract).then_inc(diffs_ready, 1)

                def sums(r):
                    if r.past(1):
                        v.wait_ge(dens_turned, r.g)
                    cm.then(nc.vector.tensor_copy(den[:, 0:1], den[:, GE:GE + 1]))
                    v.wait_ge(exps_ready, r.g + 1)
                    nc.vector.tensor_tensor_scan(den[:, 1:GE + 1], probs[:, 0, :], probs[:, 1, :], den[:, 0:1],
                                                 ALU.mult, ALU.add).then_inc(dens_ready, 1)

                def messages(r):
                    v.wait_ge(feats_done, r.g + 1)
                    for c in range(KC):
                        v.wait_ge(p_copied, r.g * 2 + c + 1)
                        nc.vector.tensor_tensor(msg[:, c, :], feat[:, c, :], pcopy[:, c, :], ALU.mult).then_inc(msgs_done, 1)

                def scans(r):
                    for c in range(KC):
                        v.wait_ge(spread, r.g * 6 + 3 + c)
                        v.wait_ge(msgs_done, r.g * 2 + c + 1)
                        nc.vector.tensor_tensor_scan(agg[:, c, :], bcast[c][:, :], msg[:, c, :], carry[:, c:c + 1],
                                                     ALU.mult, ALU.add).then_inc(scans_done, 1)
                    v.wait_ge(scans_done, r.g * 2 + 2)
                    cm.do(nc.vector.tensor_copy(carry[:, :], agg[:, :, GE - 1]))

                def inverse(r):
                    v.wait_ge(dens_turned, r.g + 1)
                    if r.past(1):
                        v.wait_ge(wide_ready, r.g)
                    if two:
                        cm.then(nc.vector.tensor_scalar(rdenT[:, :, :].rearrange("p u h -> p (u h)"), ps_den, SOFTMAX_EPS,
                                                        None, ALU.add))
                    flat = rdenT[:, :, :].rearrange("p u h -> p (u h)")
                    nc.vector.reciprocal(flat, flat if two else ps_den).then_inc(rden_ready, 1)

                def scale(r):
                    if r.past(1) and two:
                        v.wait_ge(turned_back, r.g)
                    cm.wait()
                    for c in range(KC):
                        v.wait_ge(spread, r.g * 6 + 5 + c)
                        nc.vector.tensor_tensor((yT if two else agg)[:, c, :], agg[:, c, :], bcast[c][:, :],
                                                ALU.mult).then_inc(scaled, 1)

                def elu_y(r):
                    v.wait_ge(exps, r.g + 1)
                    if r.past(1):
                        v.wait_ge(turned_back, r.g)
                    cm.then(nc.vector.scalar_tensor_tensor(out=yT[:, :, :], in0=eT[:, :, :], scalar=-1.0, in1=yb[:, :, :],
                                                           op0=ALU.add, op1=ALU.max))

                def finish_y(r):
                    nc.vector.tensor_tensor(yT[:, :, :], yT[:, :, :], dstT[r.b][:, :, :], ALU.add).then_inc(y_ready, 1)

                def affine_rows(r):
                    v.wait_ge(t_normed, r.g + 1)
                    ct.then(nc.vector.tensor_tensor(yrow[:, :, :], yrow[:, :, :], row_of(m["lnw_b"], U), ALU.mult))
                    nc.vector.tensor_tensor(yrow[:, :, :], yrow[:, :, :], row_of(m["lnb_b"], U), ALU.add).then_inc(affine, 1)

                def residual(r):
                    v.wait_ge(o_exp, r.g + 1)
                    v.wait_ge(affine, r.g + 1)
                    ct.then(nc.vector.scalar_tensor_tensor(out=yrow[:, :, :], in0=erow[:, :, :], scalar=-1.0,
                                                           in1=yrow[:, :, :], op0=ALU.add, op1=ALU.max))
                    if r.past(1):
                        v.wait_ge(u_normed, r.g)
                    nc.vector.scalar_tensor_tensor(out=y2row[:, :, :], in0=rows[r.b][:, U:2 * U, :], scalar=2.0,
                                                   in1=yrow[:, :, :], op0=ALU.mult, op1=ALU.add).then_inc(y2_done, 1)
                    v.wait_ge(y2_done, r.g + 1)
                    stats(r, st_u, y2row, U, u_stats, u_scalars)

                def lift_nodes(r):
                    v.wait_ge(d_scalars[0], r.g + 1)
                    cd.then(nc.vector.tensor_scalar(rs_d[0][:, 0, :], rs_d[0][:, 0, :], 2.0, None, ALU.mult))
                    for j in range(R):
                        t = nc.vector.scalar_tensor_tensor(out=xb[r.b][:, j, 0:F], in0=xb[r.b][:, j, 0:F],
                                                           scalar=rs_d[0][:, 0, j:j + 1], in1=m["elu_lnb"][:, :],
                                                           op0=ALU.mult, op1=ALU.add)
                    t.then_inc(x_lifted, 1)
                    v.wait_ge(x_lifted, r.g + 1)
                    stats(r, st_d[1], xb[r.b], R, d_stats[1], d_scalars[1])

                def back_stats(r):
                    v.wait_ge(turned_back, r.g + 1)
                    stats(r, st_t, back, U, t_stats, t_scalars)

                def add_rows(r):
                    v.wait_ge(x_in[r.b], (r.n + 1) * 16)
                    if r.past(2):
                        v.wait_ge(o_out[r.b], r.n * 16)
                    nc.vector.tensor_tensor(ob[r.b][:, R // 2:R, 0:F], xb[r.b][:, R // 2:R, 0:F],
                                            row_of(m["elu_bias"], R // 2), ALU.add).then_inc(v_added, 1)

                def end_stats(r, last):
                    k = 2 if two else 0
                    v.wait_ge(x_added, r.g + 1)
                    if not two:
                        v.wait_ge(v_added, r.g + 1)
                    stats(r, st_d[k], ob[r.b], R if last else R // 2, d_stats[k], d_scalars[k], R // 2 if last else 0, last)

                def front_stats(r):
                    v.wait_ge(got[r.b], (r.n + 1) * 2 * U * 16)
                    stats(r, st_f, raw[r.b], 2 * U, f_stats, f_scalars)

                def body(r):
                    for c in (cm, ct, cd):
                        c.start(r)
                    if two:
                        if r.has(0):
                            v.wait_ge(x_in[r.b], (r.n + 1) * 16)
                            stats(r, st_d[0], xb[r.b], R // 2, d_stats[0], x_lifted, 0, False)
                            inverse(r)
                            stats(r, st_d[0], xb[r.b], R, d_stats[0], x_lifted, R // 2)
                            messages(r)
                            scans(r)
                        if r.has(-1):
                            affine_rows(r.at(-1))
                        if r.has(0):
                            scale(r)
                        if r.has(2):
                            front_stats(r.at(2))
                        if r.has(-1):
                            residual(r.at(-1))
                        if r.has(0):
                            lift_nodes(r)
                        if r.has(-1):
                            end_stats(r.at(-1), False)
                        if r.has(1):
                            leaks(r.at(1))
                        if r.has(0):
                            back_stats(r)
                        if r.has(1):
                            maxima(r.at(1))
                        if r.has(-1):
                            end_stats(r.at(-1), True)
                        if r.has(1):
                            sums(r.at(1))
                    else:
                        if r.has(0):
                            inverse(r)
                        if r.has(-1):
                            end_stats(r.at(-1), True)
                        if r.has(0):
                            messages(r)
                        if r.has(-1):
                            back_stats(r.at(-1))
                        if r.has(0):
                            scans(r)
                            scale(r)
                            add_rows(r)
                        if r.has(1):
                            leaks(r.at(1))
                            maxima(r.at(1))
                        if r.has(0):
                            elu_y(r)
                        if r.has(1):
                            sums(r.at(1))
                        if r.has(0):
                            finish_y(r)
                            end_stats(r, False)
                    for c in (cm, ct, cd):
                        c.end()

                first = Round(0, 0, 0)
                for c in (cm, ct, cd):
                    c.start(first)
                if two:
                    front_stats(first)
                    front_stats(first.at(1))
                leaks(first)
                maxima(first)
                sums(first)
                for c in (cm, ct, cd):
                    c.end()
                rounds(v, body, 1)
        sem.clear()


def scatter_phase(nc, m, kept, table, tag):
    B = 4

    def turns(eng, body):
        for g in range(B):
            body(Round(g, g, 0))
        with eng.Fori(0, G // B - 1) as i:
            for k in range(B):
                body(Round(i * B + B + k, k, i + 1))
        for g in range(G // B * B, G):
            body(Round(g, g % B, g // B))

    with ExitStack() as ctx:
        sb = lambda n, shape, dt=F32: ctx.enter_context(nc.sbuf_tensor(f"{n}_{tag}", shape, dt))
        sem = Sems(nc, ctx, tag)
        rows = [sb(f"rows{i}", [P, U, W]) for i in range(B)]
        idx = [sb(f"idx{i}", [P, U], I32) for i in range(B)]
        rows_in = [sem(f"rows_in{i}") for i in range(B)]
        idx_ready, released, written = sem("idx_ready"), sem("released"), [sem(f"written{i}") for i in range(B)]
        with nc.Block() as block:
            @block.sync
            def _(sp):
                def load(r):
                    if r.past(B):
                        sp.wait_ge(written[r.b], r.n * U * 16)
                    sp.dma_start(rows[r.b][:, :, :], kept[bass.ds(r.g * GE, GE), :].rearrange("(u p) n -> p u n", p=P)
                                 ).then_inc(rows_in[r.b], 16)
                turns(sp, load)

            @block.vector
            def _(v):
                def pick(r):
                    if r.past(B):
                        v.wait_ge(written[r.b], r.n * U * 16)
                    nc.vector.tensor_copy(idx[r.b][:, :], m["last_idx"][:, bass.ds(r.g * U, U)]).then_inc(idx_ready, 1)
                turns(v, pick)

            @block.gpsimd
            def _(pool):
                bound = pool.to_reg(N - 1)

                def scatter(r):
                    pool.wait_ge(idx_ready, r.g + 1)
                    pool.wait_ge(rows_in[r.b], (r.n + 1) * 16)
                    if r.past(B):
                        pool.wait_ge(written[r.b], r.n * U * 16)
                    pool.sem_inc(released, 1)
                    for u in range(U):
                        nc.gpsimd.indirect_dma_start(
                            table[0:N, :], bass.IndirectOffsetOnAxis(ap=idx[r.b][:, u:u + 1], axis=0), rows[r.b][:, u, :], None,
                            bounds_check=bound, oob_is_err=False).then_inc(written[r.b], 16)
                turns(pool, scatter)
                for b in range(B):
                    pool.wait_ge(written[b], (G + B - 1 - b) // B * U * 16)
        sem.clear()


def add_phase(nc, m):
    ident, w1t = m["ident"], m["weights"]["w1t"]
    with ExitStack() as ctx:
        sb = lambda n, shape, dt=F32: ctx.enter_context(nc.sbuf_tensor(f"{n}_add", shape, dt))
        pb = lambda n, shape: ctx.enter_context(nc.psum_tensor(f"{n}_add", shape, F32))
        sem = Sems(nc, ctx, "add")
        two_of = lambda n, shape, dt=F32: [sb(f"{n}{i}", shape, dt) for i in range(2)]
        gidx = two_of("gidx", [P, U], I32)
        srcs = two_of("srcs", [P, GE], I32)
        wcol = two_of("wcol", [P, U])
        got_rows = two_of("got_rows", [P, U, W])
        mrow = two_of("mrow", [P, U, F])
        equal = two_of("equal", [P, U, GE])
        dup = sb("dup", [P, U, GE])
        cnt = sb("cnt", [P, 4, U])
        aidx = two_of("aidx", [P, U], I32)
        sumT = two_of("sumT", [P, KC, GE])
        adds = two_of("adds", [P, U, W])
        ps_sum = pb("ps_sum", [P, KC, GE])
        ps_add = pb("ps_add", [P, U, F])
        gidx_ready, srcs_in, got = sem("gidx_ready"), [sem(f"srcs_in{i}") for i in range(2)], [sem(f"got{i}") for i in range(2)]
        weighted, equal_ready, sums_done, sums_copied, adds_done, adds_ready, added = (
            sem("weighted"), sem("equal_ready"), sem("sums_done"), sem("sums_copied"), sem("adds_done"), sem("adds_ready"), sem("added"))
        released, marked, ch, wcol_ready = sem("released"), sem("marked"), sem("ch"), sem("wcol_ready")
        with nc.Block() as block:
            @block.gpsimd
            def _(pool):
                bound, dump_bound = pool.to_reg(EP - 1), pool.to_reg(NT - 1)

                def pick(r):
                    pool.wait_ge(gidx_ready, r.g + 1)
                    if r.past(2):
                        pool.wait_ge(weighted, r.g - 1)
                    pool.sem_inc(released, 1)

                def gather(r, u):
                    nc.gpsimd.indirect_dma_start(
                        got_rows[r.b][:, u, :], None, m["gat1_rows"], bass.IndirectOffsetOnAxis(ap=gidx[r.b][:, u:u + 1], axis=0),
                        bounds_check=bound, oob_is_err=False).then_inc(got[r.b], 16)

                def add(r):
                    pool.wait_ge(adds_ready, r.g + 1)
                    if r.past(1):
                        pool.wait_ge(added, r.g * U * 16)
                    pool.sem_inc(released, 1)
                    for u in range(U):
                        nc.gpsimd.indirect_dma_start(
                            m["node_table"], bass.IndirectOffsetOnAxis(ap=aidx[r.b][:, u:u + 1], axis=0), adds[r.b][:, u, :], None,
                            bounds_check=dump_bound, oob_is_err=True, compute_op=ALU.add).then_inc(added, 16)

                def gathers(r):
                    pick(r)
                    for u in range(U):
                        gather(r, u)

                def body(r):
                    if r.has(2):
                        gathers(r.at(2))
                    add(r)

                for r in (Round(0, 0, 0), Round(1, 1, 0)):
                    gathers(r)
                rounds(pool, body)
                pool.wait_ge(added, T * 16)

            @block.sync
            def _(sp):
                def load(r):
                    if r.past(2):
                        sp.wait_ge(equal_ready, r.g - 1)
                    sp.dma_start(srcs[r.b][:, :], m["src_rev_rows"][0:1, bass.ds(r.g * GE, GE)].partition_broadcast(P)).then_inc(srcs_in[r.b], 16)
                rounds(sp, load)

            @block.scalar
            def _(act):
                nc.scalar.preload_act_table_set("natural_log_exp_and_others")

                def weigh(r):
                    act.wait_ge(got[r.b], (r.n + 1) * U * 16)
                    act.wait_ge(wcol_ready, r.g + 1)
                    if r.past(2):
                        act.wait_ge(sums_done, (r.g - 1) * KC)
                    for u in range(U):
                        t = nc.scalar.activation(mrow[r.b][:, u, :], got_rows[r.b][:, u, 0:F], ACT.Copy,
                                                 scale=wcol[r.b][:, u:u + 1])
                    t.then_inc(weighted, 1)

                def copy_sums(r):
                    for c in range(KC):
                        act.wait_ge(sums_done, r.g * KC + c + 1)
                        if r.past(2):
                            act.wait_ge(adds_done, r.g - 1)
                        nc.scalar.activation(sumT[r.b][:, c, :], ps_sum[:, c, :], ACT.Copy).then_inc(sums_copied, 1)

                def body(r):
                    if r.has(1):
                        weigh(r.at(1))
                        copy_sums(r.at(1))

                weigh(Round(0, 0, 0))
                copy_sums(Round(0, 0, 0))
                rounds(act, body)

            @block.vector
            def _(v):
                c = Steps(v, ch)
                for b in range(2):
                    nc.vector.memset(adds[b][:, :, F:W], 0.0)
                nc.vector.memset(cnt[:, :, :], 0.0).then_inc(marked, 1)
                v.wait_ge(marked, 1)

                def picks(r):
                    if r.past(2):
                        v.wait_ge(got[r.b], r.n * U * 16)
                    nc.vector.tensor_copy(gidx[r.b][:, :], m["run_end"][:, bass.ds(r.g * U, U)]).then_inc(gidx_ready, 1)
                    if r.past(2):
                        v.wait_ge(weighted, r.g - 1)
                    nc.vector.tensor_copy(wcol[r.b][:, :], m["wrev"][:, bass.ds(r.g * U, U)]).then_inc(wcol_ready, 1)

                def equals(r):
                    v.wait_ge(srcs_in[r.b], (r.n + 1) * 16)
                    if r.past(2):
                        v.wait_ge(sums_done, (r.g - 1) * KC)
                    c.then(nc.vector.tensor_copy(cnt[:, 0, :], m["srcf_rev"][:, bass.ds(r.g * U, U)]))
                    nc.vector.tensor_tensor(equal[r.b][:, :, :], srcs[r.b][:, :].unsqueeze(1).to_broadcast([P, U, GE]),
                                            cnt[:, 0, :].unsqueeze(2).to_broadcast([P, U, GE]), ALU.is_equal).then_inc(equal_ready, 1)

                def targets(r):
                    v.wait_ge(equal_ready, r.g + 1)
                    c.then(nc.vector.tensor_tensor(dup[:, :, :], equal[r.b][:, :, :], m["later"][:, :, :], ALU.mult))
                    c.do(nc.vector.tensor_reduce(cnt[:, 1, :], dup[:, :, :], AX.X, ALU.max))
                    c.then(nc.vector.tensor_tensor(cnt[:, 2, :], m["dump"][:, :], cnt[:, 0, :], ALU.subtract))
                    c.then(nc.vector.tensor_tensor(cnt[:, 3, :], cnt[:, 2, :], cnt[:, 1, :], ALU.mult))
                    if r.past(2):
                        v.wait_ge(added, (r.g - 1) * U * 16)
                    c.do(nc.vector.tensor_tensor(aidx[r.b][:, :], cnt[:, 3, :], cnt[:, 0, :], ALU.add))
                    c.wait()

                def finish(r):
                    v.wait_ge(adds_done, r.g + 1)
                    if r.past(2):
                        v.wait_ge(added, (r.g - 1) * U * 16)
                    nc.vector.tensor_copy(adds[r.b][:, :, 0:F], ps_add[:, :, :]).then_inc(adds_ready, 1)

                def body(r):
                    c.start(r)
                    if r.has(2):
                        picks(r.at(2))
                    if r.has(1):
                        equals(r.at(1))
                    finish(r)
                    if r.has(1):
                        targets(r.at(1))
                    c.end()

                first = Round(0, 0, 0)
                c.start(first)
                picks(first)
                picks(first.at(1))
                equals(first)
                targets(first)
                c.end()
                rounds(v, body)

            @block.tensor
            def _(pe):
                def sums(r):
                    pe.wait_ge(weighted, r.g + 1)
                    pe.wait_ge(equal_ready, r.g + 1)
                    for c in range(KC):
                        if r.past(1):
                            pe.wait_ge(sums_copied, (r.g - 1) * KC + c + 1)
                        for u in range(U):
                            t = nc.tensor.matmul(ps_sum[:, c, :], mrow[r.b][:, u, c * P:(c + 1) * P], equal[r.b][:, u, :],
                                                 start=(u == 0), stop=(u == U - 1))
                        t.then_inc(sums_done, 1)

                def products(r):
                    pe.wait_ge(sums_copied, (r.g + 1) * KC)
                    if r.past(1):
                        pe.wait_ge(adds_ready, r.g)
                    for u in range(U):
                        for c in range(KC):
                            t = nc.tensor.matmul(ps_add[:, u, :], sumT[r.b][:, c, u * P:(u + 1) * P], w1t[:, c, :],
                                                 start=(c == 0), stop=(c == KC - 1))
                    t.then_inc(adds_done, 1)

                def body(r):
                    products(r)
                    if r.has(1):
                        sums(r.at(1))

                sums(Round(0, 0, 0))
                rounds(pe, body)
        sem.clear()


def last_phase(nc, m):
    ident, w3t = m["ident"], m["weights"]["w3t"]
    with ExitStack() as ctx:
        sb = lambda n, shape, dt=F32: ctx.enter_context(nc.sbuf_tensor(f"{n}_last", shape, dt))
        pb = lambda n, shape: ctx.enter_context(nc.psum_tensor(f"{n}_last", shape, F32))
        sem = Sems(nc, ctx, "last")
        two_of = lambda n, shape, dt=F32: [sb(f"{n}{i}", shape, dt) for i in range(2)]
        idx = two_of("idx", [P, 2 * U], I32)
        sidx = two_of("sidx", [P, U], I32)
        same = two_of("same", [P, GE])
        raw = two_of("raw", [P, U, W])
        own = two_of("own", [P, U, W])
        wcol = sb("wcol", [P, U])
        y2 = sb("y2", [P, U, F])
        part = sb("part", [P, U, F])
        mrow = sb("mrow", [P, U, F])
        agg = sb("agg", [P, KC, GE])
        carry = sb("carry", [P, KC])
        z = sb("z", [P, U, F])
        orow = two_of("orow", [P, U, F])
        st_ends, rs_ends = sb("st_ends", [P, 2 * U, 6]), sb("rs_ends", [P, 2, 2 * U])
        st_y2, rs_y2 = sb("st_y2", [P, U, 6]), sb("rs_y2", [P, 2, U])
        wk, half = sb("wk", [P, 6, 2 * U]), sb("half", [P, 2 * U])
        twice = sb("twice", [P, U])
        co = sb("co", [P, 4, U])
        turn = pb("turn", [P, KC, GE])
        ps_out = pb("ps_out", [P, U, F])
        idx_in, same_in, got, own_in, written = ([sem(f"{n}{i}") for i in range(2)]
                                                 for n in ("idx_in", "same_in", "got", "own_in", "written"))
        ends_stats, ends_scalars, y2_stats, y2_scalars = (
            sem(n) for n in ("ends_stats", "ends_scalars", "y2_stats", "y2_scalars"))
        lifted, co_ready, parts_ready, msgs_ready, turned, scans_done, prod_done, own_used, out_normed = (
            sem(n) for n in ("lifted", "co_ready", "parts_ready", "msgs_ready", "turned", "scans_done", "prod_done",
                             "own_used", "out_normed"))
        sidx_ready, marked, vec, pool_n, released = (sem(n) for n in ("sidx_ready", "marked", "vec", "pool_n", "released"))
        with nc.Block() as block:
            @block.gpsimd
            def _(pool):
                bound = pool.to_reg(N - 1)
                c = Steps(pool, pool_n)
                nc.gpsimd.memset(half[:, :], -0.5).then_inc(released, 1)
                pool.wait_ge(released, 1)

                def norm_y2(r):
                    pool.wait_ge(y2_stats, r.g + 1)
                    if r.past(1):
                        pool.wait_ge(co_ready, r.g)
                    norm_chain(nc, c, st_y2, wk, half, U, rs_y2, y2_scalars)
                    pool.wait_ge(y2_scalars, r.g + 1)

                def norm_ends(r):
                    pool.wait_ge(ends_stats, r.g + 3)
                    if r.has(1):
                        pool.wait_ge(lifted, r.g + 2)
                    if r.past(2):
                        pool.wait_ge(out_normed, r.g - 1)
                    norm_chain(nc, c, st_ends, wk, half, 2 * U, rs_ends, ends_scalars)
                    pool.wait_ge(ends_scalars, r.g + 3)

                def gather(r):
                    pool.wait_ge(idx_in[r.b], (r.n + 1) * 16)
                    if r.past(2):
                        pool.wait_ge(parts_ready, r.g - 1)
                    pool.sem_inc(released, 1)
                    for u in range(U):
                        nc.gpsimd.indirect_dma_start(
                            raw[r.b][:, u, :], None, m["node_table"][0:N, :],
                            bass.IndirectOffsetOnAxis(ap=idx[r.b][:, u:u + 1], axis=0),
                            bounds_check=bound, oob_is_err=False).then_inc(got[r.b], 16)

                def scatter(r):
                    pool.wait_ge(sidx_ready, r.g + 1)
                    pool.wait_ge(out_normed, r.g + 1)
                    pool.sem_inc(released, 1)
                    for u in range(U):
                        nc.gpsimd.indirect_dma_start(
                            m["out"], bass.IndirectOffsetOnAxis(ap=sidx[r.b][:, u:u + 1], axis=0), orow[r.b][:, u, :], None,
                            bounds_check=bound, oob_is_err=False).then_inc(written[r.b], 16)

                def body(r):
                    c.start(r)
                    if r.has(-2):
                        scatter(r.at(-2))
                    if r.has(1):
                        norm_y2(r.at(1))
                    if not r.static or r.g <= G:
                        norm_ends(r)
                    if r.has(3):
                        gather(r.at(3))
                    c.end()

                first = Round(0, 0, 0)
                gather(first)
                gather(first.at(1))
                c.start(first)
                pool.wait_ge(ends_stats, 1)
                norm_chain(nc, c, st_ends, wk, half, 2 * U, rs_ends, ends_scalars)
                norm_y2(first)
                pool.wait_ge(ends_stats, 2)
                pool.wait_ge(lifted, 1)
                norm_chain(nc, c, st_ends, wk, half, 2 * U, rs_ends, ends_scalars)
                pool.wait_ge(ends_scalars, 2)
                c.end()
                gather(first.at(2))
                rounds(pool, body, 2)
                for b in range(2):
                    pool.wait_ge(written[b], (G + 1 - b) // 2 * U * 16)

            @block.sync
            def _(sp):
                def load_idx(r):
                    if r.past(2):
                        sp.wait_ge(got[r.b], r.n * U * 16)
                    sp.dma_start(idx[r.b][:, :], m["pair_idx"][bass.ds(r.g, 1), :, :].rearrange("a p n -> (a p) n")
                                 ).then_inc(idx_in[r.b], 16)

                def load_rows(r):
                    if r.past(2):
                        sp.wait_ge(scans_done, r.g - 1)
                        sp.wait_ge(own_used, r.g - 1)
                    sp.dma_start(same[r.b][:, :], m["run_same"][0:1, bass.ds(r.g * GE, GE)].partition_broadcast(P)
                                 ).then_inc(same_in[r.b], 16)
                    sp.dma_start(own[r.b][:, :, :], m["gat2_rows"][bass.ds(r.g * GE, GE), :].rearrange("(u p) n -> p u n", p=P)
                                 ).then_inc(own_in[r.b], 16)

                def body(r):
                    if r.has(3):
                        load_idx(r.at(3))
                    if r.has(1):
                        load_rows(r.at(1))

                first = Round(0, 0, 0)
                load_idx(first)
                load_idx(first.at(1))
                load_rows(first)
                load_idx(first.at(2))
                rounds(sp, body)

            @block.scalar
            def _(act):
                nc.scalar.preload_act_table_set("natural_log_exp_and_others")

                def parts(r):
                    act.wait_ge(co_ready, r.g + 1)
                    if r.past(1):
                        act.wait_ge(msgs_ready, r.g)
                    for u in range(U):
                        t = nc.scalar.activation(part[:, u, :], raw[r.b][:, u, 0:F], ACT.Identity,
                                                 bias=co[:, 2, u:u + 1], scale=co[:, 0, u:u + 1])
                    t.then_inc(parts_ready, 1)

                def outputs(r):
                    act.wait_ge(ends_scalars, r.g + 4)
                    if r.past(2):
                        act.wait_ge(written[r.b], r.n * U * 16)
                    for u in range(U):
                        t = nc.scalar.activation(orow[r.b][:, u, :], z[:, u, :], ACT.Identity,
                                                 bias=rs_ends[:, 1, U + u:U + u + 1], scale=rs_ends[:, 0, U + u:U + u + 1])
                    t.then_inc(out_normed, 1)

                def body(r):
                    if r.has(-2):
                        outputs(r.at(-2))
                    if r.has(1):
                        parts(r.at(1))

                parts(Round(0, 0, 0))
                rounds(act, body, 2)

            @block.vector
            def _(v):
                c = Steps(v, vec)
                nc.vector.memset(st_ends[:, :, :], 0.0)
                nc.vector.memset(carry[:, :], 0.0).then_inc(marked, 1)
                v.wait_ge(marked, 1)

                def row_stats(r):
                    if r.past(1):
                        v.wait_ge(ends_scalars, r.g)
                    v.wait_ge(got[r.b], (r.n + 1) * U * 16)
                    for u in range(U):
                        t = nc.vector.bn_stats(st_ends[:, u, :], raw[r.b][:, u, 0:F])
                    return t

                def lift(r):
                    v.wait_ge(ends_scalars, r.g + 1)
                    c.then(nc.vector.tensor_scalar(twice[:, :], rs_ends[:, 0, 0:U], 2.0, None, ALU.mult))
                    if r.past(1):
                        v.wait_ge(msgs_ready, r.g)
                    for u in range(U):
                        t = nc.vector.scalar_tensor_tensor(out=y2[:, u, :], in0=raw[r.b][:, u, 0:F], scalar=twice[:, u:u + 1],
                                                           in1=m["elu_lnb"][:, :], op0=ALU.mult, op1=ALU.add)
                    t.then_inc(lifted, 1)
                    v.wait_ge(lifted, r.g + 1)
                    if r.past(1):
                        v.wait_ge(y2_scalars, r.g)
                    for u in range(U):
                        t = nc.vector.bn_stats(st_y2[:, u, :], y2[:, u, :])
                    t.then_inc(y2_stats, 1)

                def coefficients(r):
                    if r.past(1):
                        v.wait_ge(parts_ready, r.g)
                    c.then(nc.vector.tensor_copy(wcol[:, :], m["wcols"][:, bass.ds(r.g * U, U)]))
                    c.then(nc.vector.tensor_tensor(co[:, 0, :], wcol[:, :], raw[r.b][:, :, F], ALU.mult))
                    c.then(nc.vector.tensor_tensor(co[:, 3, :], wcol[:, :], co[:, 0, :], ALU.subtract))
                    v.wait_ge(y2_scalars, r.g + 1)
                    c.do(nc.vector.tensor_tensor(co[:, 1, :], co[:, 3, :], rs_y2[:, 0, :], ALU.mult))
                    nc.vector.tensor_tensor(co[:, 2, :], co[:, 3, :], rs_y2[:, 1, :], ALU.mult).then_inc(co_ready, 1)

                def messages(r):
                    v.wait_ge(co_ready, r.g + 1)
                    v.wait_ge(parts_ready, r.g + 1)
                    if r.past(1):
                        v.wait_ge(turned, r.g)
                    for u in range(U):
                        t = nc.vector.scalar_tensor_tensor(out=mrow[:, u, :], in0=y2[:, u, :], scalar=co[:, 1, u:u + 1],
                                                           in1=part[:, u, :], op0=ALU.mult, op1=ALU.add)
                    t.then_inc(msgs_ready, 1)
                    v.wait_ge(msgs_ready, r.g + 1)

                def sums(r):
                    v.wait_ge(same_in[r.b], (r.n + 1) * 16)
                    v.wait_ge(turned, r.g + 1)
                    if r.past(1):
                        v.wait_ge(prod_done, r.g)
                    for k in range(KC):
                        t = nc.vector.tensor_tensor_scan(agg[:, k, :], same[r.b][:, :], turn[:, k, :], carry[:, k:k + 1],
                                                         ALU.mult, ALU.add)
                    t.then_inc(scans_done, 1)
                    v.wait_ge(scans_done, r.g + 1)
                    c.then(nc.vector.tensor_copy(carry[:, :], agg[:, :, GE - 1]))

                def outputs(r):
                    if r.past(2):
                        v.wait_ge(written[r.b], r.n * U * 16)
                    nc.vector.tensor_copy(sidx[r.b][:, :], m["last_idx"][:, bass.ds(r.g * U, U)]).then_inc(sidx_ready, 1)
                    v.wait_ge(own_in[r.b], (r.n + 1) * 16)
                    v.wait_ge(prod_done, r.g + 1)
                    if r.past(1):
                        v.wait_ge(out_normed, r.g)
                    nc.vector.tensor_tensor(z[:, :, :], ps_out[:, :, :], own[r.b][:, :, 0:F], ALU.add).then_inc(own_used, 1)
                    v.wait_ge(own_used, r.g + 1)
                    c.then(nc.vector.tensor_tensor(z[:, :, :], z[:, :, :], m["b3_b"][:, :].unsqueeze(1).to_broadcast([P, U, F]), ALU.add))
                    for u in range(U):
                        t = nc.vector.bn_stats(st_ends[:, U + u, :], z[:, u, :])
                    return t

                def body(r):
                    c.start(r)
                    if r.has(1):
                        lift(r.at(1))
                    if r.has(-1):
                        last = outputs(r.at(-1))
                    if r.has(2):
                        last = row_stats(r.at(2))
                    last.then_inc(ends_stats, 1)
                    if r.has(1):
                        coefficients(r.at(1))
                    if r.has(0):
                        sums(r)
                    if r.has(1):
                        messages(r.at(1))
                    c.end()

                first = Round(0, 0, 0)
                c.start(first)
                row_stats(first).then_inc(ends_stats, 1)
                lift(first)
                row_stats(first.at(1)).then_inc(ends_stats, 1)
                coefficients(first)
                messages(first)
                c.end()
                rounds(v, body, 1)

            @block.tensor
            def _(pe):
                def turn_rows(r):
                    pe.wait_ge(msgs_ready, r.g + 1)
                    if r.past(1):
                        pe.wait_ge(scans_done, r.g)
                    for k in range(KC):
                        for u in range(U):
                            t = nc.tensor.transpose(turn[:, k, u * P:(u + 1) * P], mrow[:, u, k * P:(k + 1) * P], ident[:, :])
                    t.then_inc(turned, 1)

                def products(r):
                    pe.wait_ge(scans_done, r.g + 1)
                    if r.past(1):
                        pe.wait_ge(own_used, r.g)
                    for u in range(U):
                        for k in range(KC):
                            t = nc.tensor.matmul(ps_out[:, u, :], agg[:, k, u * P:(u + 1) * P], w3t[:, k, :],
                                                 start=(k == 0), stop=(k == KC - 1))
                    t.then_inc(prod_done, 1)

                def body(r):
                    products(r)
                    if r.has(1):
                        turn_rows(r.at(1))

                turn_rows(Round(0, 0, 0))
                rounds(pe, body)


def kernel(x, src, dst, edge_weight, L0_gnn_W_fc, L0_gnn_attn_l, L0_gnn_attn_r, L0_gnn_bias, L0_gnn_sem_W1,
           L0_gnn_sem_b1, L0_gnn_sem_W2, L1_gnn_W, L2_gnn_lin_w, L2_gnn_att, L2_gnn_ln_w, L2_gnn_ln_b, L3_gnn_W, L3_gnn_b):
    import concourse.bacc as bacc
    from concourse.bass_utils import run_bass_kernel_spmd

    c = lambda a: np.ascontiguousarray(np.asarray(a))

    def padded(a, fill):
        return np.concatenate([c(a), np.full(EP - E, fill, c(a).dtype)])

    s, d, w = padded(src, N), padded(dst, N), padded(edge_weight, 0)
    nxt = np.concatenate([d[1:], np.full(1, N + 1, d.dtype)])
    tiles = lambda a: c(a.reshape(T, P).T)
    back = lambda a: c(a[::-1].reshape(P, T))
    place = np.arange(P)[:, None] + np.arange(U)[None, :] * P
    arrays = {
        "x": c(x),
        "pair_idx": c(np.concatenate([s.reshape(G, U, P).transpose(0, 2, 1), d.reshape(G, U, P).transpose(0, 2, 1)], axis=2)),
        "dst_lin": c(d.reshape(P, T)), "dst_prev": c(np.concatenate([np.full(1, -1, d.dtype), d[:-1]]).reshape(P, T)),
        "dst_cols": tiles(d), "dst_next": tiles(nxt), "w_cols": tiles(w),
        "src_rev": back(s), "src_rev_rows": c(back(s).T.reshape(1, EP)), "dst_rev": back(d), "dst_next_rev": back(nxt),
        "w_rev": back(w), "pos_rev": back(np.arange(EP, dtype=np.float32)),
        "dump_col": (DUMP + place).astype(np.float32),
        "ident_in": np.eye(P, dtype=np.float32),
        "heads_in": (np.arange(H)[:, None, None] == (np.arange(F) // D).reshape(1, KC, P)).astype(np.float32),
        "later_in": (np.arange(GE)[None, None, :] > place[:, :, None]).astype(np.float32),
        "w_fc": c(L0_gnn_W_fc), "lin_w": c(L2_gnn_lin_w), "w1t": c(c(L1_gnn_W).T), "w3t": c(c(L3_gnn_W).T),
        "attn_l": c(L0_gnn_attn_l).reshape(1, F), "attn_r": c(L0_gnn_attn_r).reshape(1, F),
        "att": c(L2_gnn_att).reshape(1, 2 * F),
        "bias_row": c(L0_gnn_bias).reshape(1, F), "bias_cols": c(c(L0_gnn_bias).reshape(KC, P).T),
        "ln_w": c(L2_gnn_ln_w).reshape(1, F), "ln_b": c(L2_gnn_ln_b).reshape(1, F), "b3": c(L3_gnn_b).reshape(1, F),
    }
    nc = bacc.Bacc("TRN2", target_bir_lowering=False, num_devices=1)
    aps = {k: nc.dram_tensor(k + "_dram", a.shape, mybir.dt.from_np(a.dtype), kind="ExternalInput").ap()
           for k, a in arrays.items()}
    out = nc.dram_tensor("out_dram", (N, F), F32, kind="ExternalOutput").ap()
    build(nc, out=out, **aps)
    r = run_bass_kernel_spmd(nc, [{k + "_dram": a for k, a in arrays.items()}], core_ids=[0])
    return r.results[0]["out_dram"]
```
